# Optimizing a Trainium2 kernel written in Bass

```python
import numpy as np
import jax
import jax.numpy as jnp

def _softmax(x, axis=-1):
    return jax.nn.softmax(x, axis=axis)

def _gelu(x):
    return jax.nn.gelu(x, approximate=True)

def _silu(x):
    return jax.nn.silu(x)

def _sigmoid(x):
    return jax.nn.sigmoid(x)

def _layernorm(x, axis=-1, eps=1e-05):
    m = jnp.mean(x, axis=axis, keepdims=True)
    v = jnp.var(x, axis=axis, keepdims=True)
    return (x - m) / jnp.sqrt(v + eps)

def _scatter_add(tgt, idx, src, axis=0):
    return tgt.at[idx].add(src)

def _segment_sum(src, seg, n):
    return jax.ops.segment_sum(src, seg, n)
kernel_name = 'mk_dlrm_tower_d1_rec_r8_18cb6b'

def setup_inputs(seed: int=0):
    np.random.seed(seed)
    _w = jnp.asarray

    def _rec_inputs():
        import jax
        import jax.numpy as jnp
        _tk = jax.random.key(seed)
        dense_ctx = jax.random.normal(jax.random.fold_in(_tk, 190), (2048, 16), jnp.float32)
        ids = jnp.stack([jax.random.randint(jax.random.fold_in(_tk, 200 + f), (2048,), 0, v, jnp.int32) for f, v in enumerate([125000, 12500, 1000, 1000, 12500, 1250, 125000, 12500, 1000, 1250, 1250, 1000, 1250, 1250, 1250, 125000, 1000, 125000, 1250, 12500, 12500, 1000, 1000, 12500, 125000, 12500, 1250, 1250, 1000, 125000, 1000, 12500])], axis=1)
        tbl_0 = 0.05 * jax.random.normal(jax.random.fold_in(_tk, 500 + 0), (125000, 16), jnp.float32)
        tbl_1 = 0.05 * jax.random.normal(jax.random.fold_in(_tk, 500 + 1), (12500, 16), jnp.float32)
        tbl_2 = 0.05 * jax.random.normal(jax.random.fold_in(_tk, 500 + 2), (1000, 16), jnp.float32)
        tbl_3 = 0.05 * jax.random.normal(jax.random.fold_in(_tk, 500 + 3), (1000, 16), jnp.float32)
        tbl_4 = 0.05 * jax.random.normal(jax.random.fold_in(_tk, 500 + 4), (12500, 16), jnp.float32)
        tbl_5 = 0.05 * jax.random.normal(jax.random.fold_in(_tk, 500 + 5), (1250, 16), jnp.float32)
        tbl_6 = 0.05 * jax.random.normal(jax.random.fold_in(_tk, 500 + 6), (125000, 16), jnp.float32)
        tbl_7 = 0.05 * jax.random.normal(jax.random.fold_in(_tk, 500 + 7), (12500, 16), jnp.float32)
        tbl_8 = 0.05 * jax.random.normal(jax.random.fold_in(_tk, 500 + 8), (1000, 16), jnp.float32)
        tbl_9 = 0.05 * jax.random.normal(jax.random.fold_in(_tk, 500 + 9), (1250, 16), jnp.float32)
        tbl_10 = 0.05 * jax.random.normal(jax.random.fold_in(_tk, 500 + 10), (1250, 16), jnp.float32)
        tbl_11 = 0.05 * jax.random.normal(jax.random.fold_in(_tk, 500 + 11), (1000, 16), jnp.float32)
        tbl_12 = 0.05 * jax.random.normal(jax.random.fold_in(_tk, 500 + 12), (1250, 16), jnp.float32)
        tbl_13 = 0.05 * jax.random.normal(jax.random.fold_in(_tk, 500 + 13), (1250, 16), jnp.float32)
        tbl_14 = 0.05 * jax.random.normal(jax.random.fold_in(_tk, 500 + 14), (1250, 16), jnp.float32)
        tbl_15 = 0.05 * jax.random.normal(jax.random.fold_in(_tk, 500 + 15), (125000, 16), jnp.float32)
        tbl_16 = 0.05 * jax.random.normal(jax.random.fold_in(_tk, 500 + 16), (1000, 16), jnp.float32)
        tbl_17 = 0.05 * jax.random.normal(jax.random.fold_in(_tk, 500 + 17), (125000, 16), jnp.float32)
        tbl_18 = 0.05 * jax.random.normal(jax.random.fold_in(_tk, 500 + 18), (1250, 16), jnp.float32)
        tbl_19 = 0.05 * jax.random.normal(jax.random.fold_in(_tk, 500 + 19), (12500, 16), jnp.float32)
        tbl_20 = 0.05 * jax.random.normal(jax.random.fold_in(_tk, 500 + 20), (12500, 16), jnp.float32)
        tbl_21 = 0.05 * jax.random.normal(jax.random.fold_in(_tk, 500 + 21), (1000, 16), jnp.float32)
        tbl_22 = 0.05 * jax.random.normal(jax.random.fold_in(_tk, 500 + 22), (1000, 16), jnp.float32)
        tbl_23 = 0.05 * jax.random.normal(jax.random.fold_in(_tk, 500 + 23), (12500, 16), jnp.float32)
        tbl_24 = 0.05 * jax.random.normal(jax.random.fold_in(_tk, 500 + 24), (125000, 16), jnp.float32)
        tbl_25 = 0.05 * jax.random.normal(jax.random.fold_in(_tk, 500 + 25), (12500, 16), jnp.float32)
        tbl_26 = 0.05 * jax.random.normal(jax.random.fold_in(_tk, 500 + 26), (1250, 16), jnp.float32)
        tbl_27 = 0.05 * jax.random.normal(jax.random.fold_in(_tk, 500 + 27), (1250, 16), jnp.float32)
        tbl_28 = 0.05 * jax.random.normal(jax.random.fold_in(_tk, 500 + 28), (1000, 16), jnp.float32)
        tbl_29 = 0.05 * jax.random.normal(jax.random.fold_in(_tk, 500 + 29), (125000, 16), jnp.float32)
        tbl_30 = 0.05 * jax.random.normal(jax.random.fold_in(_tk, 500 + 30), (1000, 16), jnp.float32)
        tbl_31 = 0.05 * jax.random.normal(jax.random.fold_in(_tk, 500 + 31), (12500, 16), jnp.float32)
        _rk = jax.random.fold_in(_tk, 7)
        W_top1 = 0.0693375 * jax.random.normal(jax.random.fold_in(_tk, 801), (208, 512), jnp.float32)
        W_top2 = 0.0441942 * jax.random.normal(jax.random.fold_in(_tk, 802), (512, 256), jnp.float32)
        W_top3 = 0.0625 * jax.random.normal(jax.random.fold_in(_tk, 803), (256, 1), jnp.float32)
        b_top1 = jnp.zeros((512,), jnp.float32)
        b_top2 = jnp.zeros((256,), jnp.float32)
        return (dense_ctx, ids, tbl_0, tbl_1, tbl_2, tbl_3, tbl_4, tbl_5, tbl_6, tbl_7, tbl_8, tbl_9, tbl_10, tbl_11, tbl_12, tbl_13, tbl_14, tbl_15, tbl_16, tbl_17, tbl_18, tbl_19, tbl_20, tbl_21, tbl_22, tbl_23, tbl_24, tbl_25, tbl_26, tbl_27, tbl_28, tbl_29, tbl_30, tbl_31, W_top1, b_top1, W_top2, b_top2, W_top3)
    dense_ctx, ids, tbl_0, tbl_1, tbl_2, tbl_3, tbl_4, tbl_5, tbl_6, tbl_7, tbl_8, tbl_9, tbl_10, tbl_11, tbl_12, tbl_13, tbl_14, tbl_15, tbl_16, tbl_17, tbl_18, tbl_19, tbl_20, tbl_21, tbl_22, tbl_23, tbl_24, tbl_25, tbl_26, tbl_27, tbl_28, tbl_29, tbl_30, tbl_31, W_top1, b_top1, W_top2, b_top2, W_top3 = _rec_inputs()

    def _L0_rec_setup():
        import jax, jax.numpy as jnp
        import numpy as np
        B, M, D = (2048, 32, 16)
        LAYERS = [64, 64, 64]
        key = jax.random.key(seed)
        ks = jax.random.split(key, 4)
        inp = {'embeddings': jax.random.normal(ks[0], (B, M, D), dtype=jnp.float32)}
        hk_1 = M
        for i, hk in enumerate(LAYERS):
            scale = (2.0 / (M * hk_1 + hk)) ** 0.5
            inp[f'W{i}'] = jax.random.normal(ks[i + 1], (M, hk_1, hk), dtype=jnp.float32) * scale
            hk_1 = hk
        return inp
    _L0_rec_all = _L0_rec_setup()
    _L0_rec_in = {k: v for k, v in _L0_rec_all.items() if k in ('W0', 'W1', 'W2')}
    del _L0_rec_all
    return {'dense_ctx': dense_ctx, 'ids': ids, 'tbl_0': tbl_0, 'tbl_1': tbl_1, 'tbl_2': tbl_2, 'tbl_3': tbl_3, 'tbl_4': tbl_4, 'tbl_5': tbl_5, 'tbl_6': tbl_6, 'tbl_7': tbl_7, 'tbl_8': tbl_8, 'tbl_9': tbl_9, 'tbl_10': tbl_10, 'tbl_11': tbl_11, 'tbl_12': tbl_12, 'tbl_13': tbl_13, 'tbl_14': tbl_14, 'tbl_15': tbl_15, 'tbl_16': tbl_16, 'tbl_17': tbl_17, 'tbl_18': tbl_18, 'tbl_19': tbl_19, 'tbl_20': tbl_20, 'tbl_21': tbl_21, 'tbl_22': tbl_22, 'tbl_23': tbl_23, 'tbl_24': tbl_24, 'tbl_25': tbl_25, 'tbl_26': tbl_26, 'tbl_27': tbl_27, 'tbl_28': tbl_28, 'tbl_29': tbl_29, 'tbl_30': tbl_30, 'tbl_31': tbl_31, 'W_top1': W_top1, 'b_top1': b_top1, 'W_top2': W_top2, 'b_top2': b_top2, 'W_top3': W_top3, 'L0_rec_W0': _L0_rec_in['W0'], 'L0_rec_W1': _L0_rec_in['W1'], 'L0_rec_W2': _L0_rec_in['W2']}

def reference(dense_ctx, ids, tbl_0, tbl_1, tbl_2, tbl_3, tbl_4, tbl_5, tbl_6, tbl_7, tbl_8, tbl_9, tbl_10, tbl_11, tbl_12, tbl_13, tbl_14, tbl_15, tbl_16, tbl_17, tbl_18, tbl_19, tbl_20, tbl_21, tbl_22, tbl_23, tbl_24, tbl_25, tbl_26, tbl_27, tbl_28, tbl_29, tbl_30, tbl_31, W_top1, b_top1, W_top2, b_top2, W_top3, L0_rec_W0, L0_rec_W1, L0_rec_W2):
    import jax
    import jax.numpy as jnp

    def _L0_rec_ref(embeddings, W0, W1, W2):
        import jax, jax.numpy as jnp
        import numpy as np
        B, M, D = (2048, 32, 16)
        LAYERS = [64, 64, 64]
        x0 = embeddings
        xk = x0
        outs = []
        for W in (W0, W1, W2):
            xk = jax.nn.relu(jnp.einsum('bmd,bhd,mhk->bkd', x0, xk, W))
            outs.append(jnp.sum(xk, axis=2))
        return jnp.concatenate(outs, axis=1)
    e = jnp.stack([tbl_0[ids[:, 0]], tbl_1[ids[:, 1]], tbl_2[ids[:, 2]], tbl_3[ids[:, 3]], tbl_4[ids[:, 4]], tbl_5[ids[:, 5]], tbl_6[ids[:, 6]], tbl_7[ids[:, 7]], tbl_8[ids[:, 8]], tbl_9[ids[:, 9]], tbl_10[ids[:, 10]], tbl_11[ids[:, 11]], tbl_12[ids[:, 12]], tbl_13[ids[:, 13]], tbl_14[ids[:, 14]], tbl_15[ids[:, 15]], tbl_16[ids[:, 16]], tbl_17[ids[:, 17]], tbl_18[ids[:, 18]], tbl_19[ids[:, 19]], tbl_20[ids[:, 20]], tbl_21[ids[:, 21]], tbl_22[ids[:, 22]], tbl_23[ids[:, 23]], tbl_24[ids[:, 24]], tbl_25[ids[:, 25]], tbl_26[ids[:, 26]], tbl_27[ids[:, 27]], tbl_28[ids[:, 28]], tbl_29[ids[:, 29]], tbl_30[ids[:, 30]], tbl_31[ids[:, 31]]], axis=1)
    z = _L0_rec_ref(e, L0_rec_W0, L0_rec_W1, L0_rec_W2)
    z = z.reshape(z.shape[0], -1)
    h = jnp.concatenate([z, dense_ctx], axis=1)
    h = jnp.maximum(h @ W_top1 + b_top1, 0.0)
    h = jnp.maximum(h @ W_top2 + b_top2, 0.0)
    y = h @ W_top3
    return y

_drawn_inputs = setup_inputs


def setup_inputs(seed=0):
    import zlib

    import numpy as np

    out = dict(_drawn_inputs(seed))
    spreads = {'b_top1': (0.0, 2.0), 'b_top2': (0.0, 0.8)}
    factors = {'tbl_0': 8.0,
     'tbl_1': 8.0,
     'tbl_2': 8.0,
     'tbl_3': 8.0,
     'tbl_4': 8.0,
     'tbl_5': 8.0,
     'tbl_6': 8.0,
     'tbl_7': 8.0,
     'tbl_8': 8.0,
     'tbl_9': 8.0,
     'tbl_10': 8.0,
     'tbl_11': 8.0,
     'tbl_12': 8.0,
     'tbl_13': 8.0,
     'tbl_14': 8.0,
     'tbl_15': 8.0,
     'tbl_16': 8.0,
     'tbl_17': 8.0,
     'tbl_18': 8.0,
     'tbl_19': 8.0,
     'tbl_20': 8.0,
     'tbl_21': 8.0,
     'tbl_22': 8.0,
     'tbl_23': 8.0,
     'tbl_24': 8.0,
     'tbl_25': 8.0,
     'tbl_26': 8.0,
     'tbl_27': 8.0,
     'tbl_28': 8.0,
     'tbl_29': 8.0,
     'tbl_30': 8.0,
     'tbl_31': 8.0,
     'L0_rec_W0': 3.395,
     'L0_rec_W1': 8.0,
     'L0_rec_W2': 8.0,
     'dense_ctx': 7.29}
    for name, (base, spread) in spreads.items():
        noise = np.random.default_rng([zlib.crc32(name.encode()), seed]).standard_normal(out[name].shape)
        drawn = base * np.exp(spread * noise) if base else spread * noise
        out[name] = jnp.asarray(drawn.astype(out[name].dtype))
    for name, factor in factors.items():
        out[name] = (out[name] * factor).astype(out[name].dtype)
    return out
```

```python
from contextlib import ExitStack

import concourse.bass as bass
import numpy as np
from concourse import mybir

FP32 = mybir.dt.float32
F32R = mybir.dt.float32r
I32 = mybir.dt.int32
U32 = mybir.dt.uint32
ACT = mybir.ActivationFunctionType
ALU = mybir.AluOpType
AX = mybir.AxisListType

B, M, D, K = 2048, 32, 16, 64
NB = 128
BT = B // NB
BLK = 512
PAIRS = B * D // (2 * BLK)
H1, H2 = 512, 256
ND = 16
SHIFT_TILES = 5
NT = M * K // 128
UNITS = NT
PBUF = 8
PREP = D * NB // BLK
SQUARES = 2 * SHIFT_TILES
MLP = 3

STEP0, UNROLL, LOOPS = 3, 4, 6
LAST = PAIRS

PREP_SLOT = {1 + e: e for e in range(PREP)}
SQ_SLOT = {5 + 2 * n: (n // 2, n % 2) for n in range(SQUARES)}
L0_SLOT = {9 + 4 * t: t for t in range(SHIFT_TILES)}
MLP1_SLOT = {24 + m: m for m in range(4)}
MLP2_SLOT, MLP3_SLOT = 29, 31
X3_SLOT, X2_SLOT, X1_SLOT = 2, 18, 26
SPLIT_HIGH_SLOT, SPLIT_LOW_SLOT = 22, 25


def is_int(x):
    return isinstance(x, int)


def within(x, low, high):
    return not is_int(x) or low <= x <= high


class Step:

    def __init__(self, c, k):
        self.c, self.k = c, k
        self.s = UNROLL * c + (STEP0 + k)
        self.b = 2 * c + (STEP0 + k) // 2
        self.odd = (STEP0 + k) % 2
        first = is_int(self.s) and self.s < 2
        per = PREP + MLP + 2 * SQUARES
        self.event = self.b * per + PREP + SQUARES + (self.odd * SQUARES) - (0 if first else MLP)

    def of_parity(self, d):
        return self.c + ((STEP0 + self.k) // 2 + d) // 2 + 1

    def pair_parity(self, d):
        return (STEP0 + self.k + d) % 2

    def tile_parity(self, d=0):
        return ((STEP0 + self.k + d) // 2) % 2

    def stage(self, layer):
        s = self.s
        if layer == 1:
            if not within(s, 0, PAIRS - 1):
                return None
            base = 0 if is_int(s) and s == 0 else 2 * UNITS * s - UNITS
            return Stage(1, s, self.pair_parity(0), self.tile_parity(0), base)
        if not within(s, 1, LAST):
            return None
        base = 2 * UNITS * s - (UNITS if is_int(s) and s == LAST else 0)
        return Stage(2, s - 1, self.pair_parity(-1), self.tile_parity(-1), base)


class Stage:
    def __init__(self, layer, pair, pair_parity, tile_parity, base):
        self.layer, self.pair, self.base = layer, pair, base
        self.pp, self.tp = pair_parity, tile_parity


def quads(sg):
    if is_int(sg.base):
        return sg.base // 2
    return UNITS * (sg.pair + 1) if sg.layer == 2 else UNITS * sg.pair - UNITS // 2


def peeled(s):
    return Step((s - STEP0) // UNROLL, (s - STEP0) % UNROLL)


def run_steps(eng, one_step):
    for s in range(STEP0):
        one_step(None, peeled(s))
    with eng.Fori(0, LOOPS) as c:
        for k in range(UNROLL):
            one_step(c, Step(c, k))
    for s in range(STEP0 + UNROLL * LOOPS, LAST + 1):
        one_step(None, peeled(s))


def neighbour(c, step, d):
    if c is None:
        s = step.s + d
        return peeled(s) if 0 <= s <= LAST else None
    return Step(c, step.k + d)


def tower(nc, dense, ids, tables, w_top1, b_top1, w_top2, b_top2, w_top3, w0, w1, w2,
          sel_rows, sel_sums, identity, out):
    with ExitStack() as ctx:
        def sb(name, shape, dt=FP32):
            return ctx.enter_context(nc.sbuf_tensor(name, shape, dt))

        def pb(name, shape):
            return ctx.enter_context(nc.psum_tensor(name, shape, FP32))

        def sem(name):
            return ctx.enter_context(nc.semaphore(name))

        ident = sb("ident", [128, 128])
        rows_raw = sb("rows_raw", [128, NT // 2, 128])
        rows = sb("rows", [128, NT // 2, 128], F32R)
        sums_raw = sb("sums_raw", [64, SHIFT_TILES, 128])
        sums = sb("sums", [64, SHIFT_TILES, 128], F32R)
        w0_mh = sb("w0_mh", [128, SHIFT_TILES, K])
        w0_hm = sb("w0_hm", [128, 4, K])
        w0_rows = sb("w0_rows", [M, M, K])
        w0_cols = sb("w0_cols", [M, M, K])
        w0_sum = sb("w0_sum", [M, 3, K])
        w0_pair = sb("w0_pair", [128, 4, K])
        u = sb("u", [128, SHIFT_TILES, K])
        wk = {1: sb("w1s", [128, NT, K]), 2: sb("w2s", [128, NT, K])}
        wt_a = sb("wt_a", [128, H1])
        wt_b = sb("wt_b", [128, H1])
        wt_c = sb("wt_c", [ND + 1, H1])
        wt2 = sb("wt2", [128, H1 // 128, H2])
        wt3 = sb("wt3", [128, H2 // 128])
        bt2 = sb("bt2", [128, H2 // 128])
        dense_in = sb("dense_in", [128, BT, ND + 1])
        dense_t = sb("dense_t", [ND + 1, B])

        idx = [sb(f"idx{i}", [128, M], I32) for i in range(2)]
        emb = sb("emb", [128, M, D])
        parts = sb("parts", [128, D, 2, 2, M], F32R)
        x0 = [sb(f"x0_{i}", [128, D * NB], F32R) for i in range(2)]
        sq = [[sb(f"sq{i}{h}", [128, BLK]) for h in "ab"] for i in range(2)]
        xk = {l: [[sb(f"x{l}_{i}{h}", [128, BLK]) for h in "ab"] for i in range(2)] for l in (1, 2)}
        x3 = [sb(f"x3_{i}", [128, BLK]) for i in range(2)]
        prod = sb("prod", [128, PBUF, 2, BLK])
        z = {l: [sb(f"z{l}_{i}", [64 * l, BLK]) for i in range(2)] for l in (1, 2)}
        zt = {l: sb(f"zt{l}", [64 * l, BLK]) for l in (1, 2)}
        z3 = sb("z3", [128, BLK])
        zh = {l: sb(f"zh{l}", [64 if l == 1 else 128, 2 * NB]) for l in (1, 2, 3)}
        zr12, zr3 = sb("zr12", [128, NB]), sb("zr3", [128, NB])
        h1 = sb("h1", [128, H1 // 128, NB])
        h2 = sb("h2", [128, H2 // 128, NB])
        y = sb("y", [1, B])

        wide = pb("wide", [128, 2, 2, BLK])
        acc = [pb(f"acc{l}", [128, BLK]) for l in range(3)]
        exch = pb("exch", [128, BLK])

        s_ids = [sem(f"ids_loaded{i}") for i in range(2)]
        s_const = sem("consts_loaded")
        s_w0 = sem("w0_loaded")
        s_w12 = sem("w12_loaded")
        s_wtop = sem("wtop_loaded")
        s_gather = sem("gathered")
        s_go = sem("gather_may_start")
        s_sel = sem("selectors_ready")
        s_ones = sem("ones_ready")
        s_prep = sem("w0_steps")
        s_u = sem("u_ready")
        s_dtr = sem("dense_transposed")
        s_dt = sem("dense_t_ready")
        s_high = sem("high_ready")
        s_low = sem("low_ready")
        s_ev = sem("event_ready")
        s_taken = sem("event_taken")
        s_l0 = sem("l0_tile_done")
        s_wide = sem("wide_ready")
        s_prod = sem("prod_ready")
        s_quad = sem("quad_done")
        s_x = {1: sem("x1_ready"), 2: sem("x2_ready"), 3: sem("x3_ready")}
        s_zm = {1: sem("z1_second"), 2: sem("z2_second")}
        s_z = {1: sem("z1_summed"), 2: sem("z2_summed"), 3: sem("z3_summed")}
        s_half = sem("z_halved")
        s_zr = sem("z_reduced")
        s_y = sem("y_ready")
        s_out = sem("out_stored")

        w0_flat = w0.rearrange("m h k -> (m h) k")

        def w0_pieces():
            for s in range(M // 2 + 1):
                t, p = s // 4, 32 * (s % 4)
                for lo, hi, wrap in ((0, M - s, 0), (M - s, M, M)):
                    if hi == lo:
                        continue
                    first = lo * M + lo + s - wrap
                    n = hi - lo
                    yield (w0_mh[p + lo:p + hi, t, :], w0_flat[first:first + (M + 1) * (n - 1) + 1:M + 1, :])
                    if 0 < s < M // 2:
                        first = (lo + s - wrap) * M + lo
                        yield (w0_hm[p + lo:p + hi, t, :],
                               w0_flat[first:first + (M + 1) * (n - 1) + 1:M + 1, :])
        W0_DMAS = len(list(w0_pieces())) + 2

        block = ctx.enter_context(nc.Block())

        @block.sync
        def _(sp):
            def load_ids(b, par):
                sp.dma_start(idx[par][:, :], ids[bass.ds(b * NB, NB), :]).then_inc(s_ids[par], 16)

            load_ids(0, 0)
            load_ids(1, 1)
            sp.dma_start(dense_in[:, :, 0:ND], dense.rearrange("(t p) f -> p t f", p=NB)).then_inc(s_const, 16)
            sp.dma_start(ident[:, :], identity).then_inc(s_const, 16)
            sp.dma_start(rows_raw[:, :, :], sel_rows).then_inc(s_const, 16)
            sp.dma_start(sums_raw[:, :, :], sel_sums).then_inc(s_const, 16)
            for l, w in ((1, w1), (2, w2)):
                for mi in range(2):
                    sp.dma_start(wk[l][64 * mi:64 * mi + 64, :, :],
                                 w.rearrange("(i two) h k -> two h i k", two=2)[mi]).then_inc(s_w12, 16)
            sp.dma_start(wt_a[:, :], w_top1[0:2 * K, :]).then_inc(s_wtop, 16)
            for h in range(2):
                sp.dma_start(wt_b[64 * h:64 * h + 64, :], w_top1[2 * K:3 * K, :]).then_inc(s_wtop, 16)
            sp.dma_start(wt_c[0:ND, :], w_top1[3 * K:3 * K + ND, :]).then_inc(s_wtop, 16)
            sp.dma_start(wt_c[ND:ND + 1, :], b_top1.rearrange("(a n) -> a n", a=1)).then_inc(s_wtop, 16)
            sp.dma_start(wt2[:, :, :], w_top2.rearrange("(k p) n -> p k n", p=128)).then_inc(s_wtop, 16)
            sp.dma_start(wt3[:, :], w_top3.rearrange("(k p) n -> p (k n)", p=128),
                         allow_slow_non_contiguous=True).then_inc(s_wtop, 16)
            sp.dma_start(bt2[:, :], b_top2.rearrange("(k p) -> p k", p=128),
                         allow_slow_non_contiguous=True).then_inc(s_wtop, 16)

            sp.wait_ge(s_gather, 16 * M)
            load_ids(2, 0)

            def tile_traffic(b, par, load):
                if load:
                    sp.wait_ge(s_gather, 16 * M * (b + 2))
                    load_ids(b + 3, 1 - par)
                sp.wait_ge(s_y, b + 1)
                sp.dma_start(out.rearrange("b one -> one b")[:, bass.ds(b * NB, NB)], y[:, bass.ds(b * NB, NB)])\
                    .then_inc(s_out, 16)

            with sp.Fori(0, BT - 4, 2) as b:
                tile_traffic(b, 0, True)
                tile_traffic(b + 1, 1, True)
            for b in range(BT - 4, BT):
                tile_traffic(b, b % 2, b + 3 < BT)
            sp.wait_ge(s_out, 16 * BT)

        @block.gpsimd
        def _(pool):
            def gather(b, par, nth, lo, hi):
                if lo == 0:
                    pool.wait_ge(s_ids[par], 16 * nth)
                    if not is_int(b) or b > 0:
                        pool.wait_ge(s_low, b)
                        pool.wait_ge(s_high, b)
                pool.sem_inc(s_go, 1)
                for m in range(lo, hi):
                    pool.indirect_dma_start(
                        emb[:, m, :], None, tables[m],
                        bass.IndirectOffsetOnAxis(ap=idx[par][:, m:m + 1].bitcast(U32), axis=0)
                    ).then_inc(s_gather, 16)

            def z_of_layer(l, pair, pp, tp, b):
                p = 64 * l
                a_half, b_half = xk[l][pp][0][0:p, :], xk[l][pp][1][0:p, :]
                pool.wait_ge(s_x[l], pair + 1)
                if pp == 0:
                    if not is_int(b) or b >= 2:
                        pool.wait_ge(s_half, 3 * (b - 1))
                    pool.tensor_tensor(z[l][tp][:, :], a_half, b_half, ALU.add).then_inc(s_z[l], 1)
                else:
                    pool.tensor_tensor(zt[l][:, :], a_half, b_half, ALU.add).then_inc(s_zm[l], 1)
                    pool.wait_ge(s_zm[l], b + 1)
                    pool.wait_ge(s_z[l], pair)
                    pool.tensor_tensor(z[l][tp][:, :], z[l][tp][:, :], zt[l][:, :], ALU.add).then_inc(s_z[l], 1)

            def z_reduce(b, tp):
                pool.wait_ge(s_x[3], 2 * b + 2)
                pool.tensor_tensor(z3[:, :], x3[0][:, :], x3[1][:, :], ALU.add).then_inc(s_z[3], 1)
                pool.wait_ge(s_z[1], 2 * b + 2)
                pool.wait_ge(s_z[2], 2 * b + 2)
                pool.wait_ge(s_z[3], b + 1)
                for l, zl in ((1, z[1][tp]), (2, z[2][tp]), (3, z3)):
                    pool.tensor_tensor(zh[l][:, :], zl[:, 0:2 * NB], zl[:, 2 * NB:4 * NB], ALU.add).then_inc(s_half, 1)
                pool.wait_ge(s_half, 3 * b + 3)
                pool.tensor_tensor(zr12[:, :], zh[2][:, 0:NB], zh[2][:, NB:2 * NB], ALU.add).then_inc(s_zr, 1)
                pool.tensor_tensor(zr3[:, :], zh[3][:, 0:NB], zh[3][:, NB:2 * NB], ALU.add).then_inc(s_zr, 1)
                pool.wait_ge(s_zr, 3 * b + 2)
                pool.tensor_tensor(zr12[0:64, :], zh[1][:, 0:NB], zh[1][:, NB:2 * NB], ALU.add).then_inc(s_zr, 1)
                pool.wait_ge(s_zr, 3 * b + 3)

            pool.memset(dense_in[:, :, ND:ND + 1], 1.0).then_inc(s_ones, 1)
            gather(0, 0, 1, 0, M)
            gather(1, 1, 1, 0, M // 2)
            z_of_layer(1, 0, 0, 0, 0)

            def one_step(c, st):
                s, b = st.s, st.b
                if st.odd:
                    if within(b, 1, BT):
                        z_reduce(b - 1, st.tile_parity(-2))
                    if within(b, 0, BT - 3):
                        gather(b + 2, st.tile_parity(), st.of_parity(2), 0, M // 2)
                else:
                    if within(b, 2, BT):
                        pool.wait_ge(s_y, b - 1)
                    if within(b, 0, BT - 2):
                        gather(b + 1, st.tile_parity(2), None, M // 2, M)
                if within(s, 0, PAIRS - 1):
                    z_of_layer(2, s, st.pair_parity(0), st.tile_parity(), b)
                if within(s, 0, PAIRS - 2):
                    z_of_layer(1, s + 1, st.pair_parity(1), st.tile_parity(1), b + st.odd)

            run_steps(pool, one_step)
            pool.wait_ge(s_y, BT - 1)
            z_reduce(BT - 1, (BT - 1) % 2)

        @block.scalar
        def _(act):
            for dst, src in w0_pieces():
                act.dma_start(dst, src).then_inc(s_w0, 16)
            act.dma_start(w0_rows[:, :, :], w0).then_inc(s_w0, 16)
            act.dma_start(w0_cols[:, :, :], w0.rearrange("m h k -> h m k")).then_inc(s_w0, 16)

            def split_high(b):
                act.wait_ge(s_gather, 16 * M * (b + 1))
                nc.scalar.copy(parts[:, :, :, 0, :],
                               emb[:, :, :].rearrange("p m d -> p d m").unsqueeze(2)
                               .to_broadcast([128, D, 2, M])).then_inc(s_high, 1)

            def prep_event(e, n, tp):
                act.wait_ge(s_ev, e + 1)
                nc.scalar.copy(x0[tp][:, n * BLK:(n + 1) * BLK], exch[:, :]).then_inc(s_taken, 1)

            def square_event(e, t, half, pair):
                p = 128 if t < SHIFT_TILES - 1 else 32
                if t >= 2:
                    act.wait_ge(s_l0, SHIFT_TILES * pair + t - 1)
                elif not is_int(pair) or pair > 0:
                    act.wait_ge(s_l0, SHIFT_TILES * pair - t)
                act.wait_ge(s_ev, e + 1)
                nc.scalar.activation(sq[t % 2][half][0:p, :], exch[0:p, :], ACT.Square).then_inc(s_taken, 1)

            def evacuate(layer, pair, pp, tile):
                nxt = layer + 1
                if layer == 0:
                    act.wait_ge(s_l0, SHIFT_TILES * (pair + 1))
                else:
                    act.wait_ge(s_quad, stage_end(layer, pair) // 2 if is_int(pair)
                                else stage_end(layer, pair, 2))
                if nxt == 3:
                    if pp == 0 and not (is_int(pair) and pair < 2):
                        act.wait_ge(s_z[3], tile)
                    nc.scalar.activation(x3[pp][:, :], acc[2][:, :], ACT.Relu).then_inc(s_x[3], 1)
                    return
                if not is_int(pair) or pair >= 2:
                    act.wait_ge(s_prod, stage_end(nxt, pair - 2))
                    act.wait_ge(s_z[nxt], pair - 1)
                for half in range(2):
                    for copy in range(2):
                        last = nc.scalar.activation(xk[nxt][pp][half][64 * copy:64 * copy + 64, :],
                                                    acc[layer][64 * half:64 * half + 64, :], ACT.Relu)
                last.then_inc(s_x[nxt], 1)

            def stage_end(layer, pair, per=1):
                n = UNITS // per
                if layer == 1:
                    return n if is_int(pair) and pair == 0 else 2 * n * pair
                return 2 * n * (pair + 1) + (0 if is_int(pair) and pair == PAIRS - 1 else n)

            def mlp_event(e, n, b):
                act.wait_ge(s_ev, e + 1)
                if n == 0:
                    nc.scalar.activation(h1[:, :, :], exch[:, :].rearrange("p (m b) -> p m b", b=NB),
                                         ACT.Relu).then_inc(s_taken, 1)
                elif n == 1:
                    for j in range(H2 // 128):
                        last = nc.scalar.activation(h2[:, j, :], exch[:, j * NB:(j + 1) * NB], ACT.Relu,
                                                    bias=bt2[:, j:j + 1])
                    last.then_inc(s_taken, 1)
                else:
                    nc.scalar.copy(y[:, bass.ds(b * NB, NB)], exch[0:1, 0:NB]).then_inc(s_taken, 1)
                    act.wait_ge(s_taken, e + 1)
                    act.sem_inc(s_y, 1)

            split_high(0)
            for n in range(PREP):
                prep_event(n, n, 0)
            for t in range(SHIFT_TILES):
                for half in range(2):
                    square_event(PREP + 2 * t + half, t, half, 0)
            evacuate(0, 0, 0, 0)
            act.wait_ge(s_wtop, 16 * 8)

            def one_step(c, st):
                s, b, e = st.s, st.b, st.event
                for slot in range(2 * UNITS):
                    if st.odd and slot in PREP_SLOT and within(b, 0, BT - 2):
                        prep_event(e, PREP_SLOT[slot], st.tile_parity(2))
                        e = e + 1
                    if slot in SQ_SLOT and within(s, 0, PAIRS - 2):
                        square_event(e, *SQ_SLOT[slot], s + 1)
                        e = e + 1
                    if st.odd and within(b, 1, BT):
                        n = {max(MLP1_SLOT): 0, MLP2_SLOT: 1, MLP3_SLOT: 2}.get(slot)
                        if n is not None:
                            mlp_event(e, n, b - 1)
                            e = e + 1
                    if slot == X3_SLOT and within(s, 2, LAST):
                        evacuate(2, s - 2, st.pair_parity(0), b - 1)
                    if slot == X2_SLOT and within(s, 0, PAIRS - 1):
                        evacuate(1, s, st.pair_parity(0), b)
                    if slot == X1_SLOT and within(s, 0, PAIRS - 2):
                        evacuate(0, s + 1, st.pair_parity(1), b + st.odd)
                    if slot == SPLIT_HIGH_SLOT and not st.odd and within(b, 0, BT - 2):
                        split_high(b + 1)

            run_steps(act, one_step)
            evacuate(2, PAIRS - 1, 1, BT - 1)
            e = peeled(PAIRS - 1).event + MLP
            for n in range(MLP):
                mlp_event(e + n, n, BT - 1)

        @block.vector
        def _(dve):
            dve.wait_ge(s_const, 16 * 4)
            nc.vector.tensor_copy(rows[:, :, :], rows_raw[:, :, :]).then_inc(s_sel, 1)
            nc.vector.tensor_copy(sums[:, :, :], sums_raw[:, :, :]).then_inc(s_sel, 1)
            dve.wait_ge(s_w0, 16 * W0_DMAS)
            nc.vector.tensor_reduce(w0_sum[:, 0, :], w0_rows[:, :, :].rearrange("p h k -> p k h"), AX.X,
                                    ALU.add).then_inc(s_prep, 1)
            nc.vector.tensor_reduce(w0_sum[:, 1, :], w0_cols[:, :, :].rearrange("p h k -> p k h"), AX.X,
                                    ALU.add).then_inc(s_prep, 1)
            dve.wait_ge(s_prep, 2)
            nc.vector.tensor_tensor(w0_sum[:, 2, :], w0_sum[:, 0, :], w0_sum[:, 1, :], ALU.add).then_inc(s_prep, 1)
            dve.wait_ge(s_prep, 3)
            nc.vector.scalar_tensor_tensor(out=w0_hm[0:M, 0, :], in0=w0_mh[0:M, 0, :], scalar=3.0,
                                           in1=w0_sum[:, 2, :], op0=ALU.mult, op1=ALU.subtract).then_inc(s_prep, 1)
            dve.wait_ge(s_prep, 4)
            nc.vector.tensor_tensor(w0_pair[:, :, :], w0_mh[:, 0:4, :], w0_hm[:, :, :], ALU.add).then_inc(s_prep, 1)
            dve.wait_ge(s_prep, 5)
            nc.vector.tensor_scalar(u[:, 0:4, :], w0_pair[:, :, :], 0.5, None, ALU.mult).then_inc(s_u, 1)
            nc.vector.tensor_scalar(u[0:M, 4, :], w0_mh[0:M, 4, :], 0.5, None, ALU.mult).then_inc(s_u, 1)
            dve.wait_ge(s_dtr, 1)
            nc.vector.tensor_copy(dense_t[:, :], wide[0:ND + 1, :, :, :].rearrange("p a b c -> p (a b c)"))\
                .then_inc(s_dt, 1)

            def split_low(b):
                dve.wait_ge(s_high, b + 1)
                nc.vector.tensor_tensor(parts[:, :, :, 1, :],
                                        emb[:, :, :].rearrange("p m d -> p d m").unsqueeze(2)
                                        .to_broadcast([128, D, 2, M]),
                                        parts[:, :, :, 0, :].bitcast(FP32), ALU.subtract).then_inc(s_low, 1)

            split_low(0)

            def products(sg, i):
                g = sg.base + i
                if i == 0:
                    dve.wait_ge(s_x[sg.layer], sg.pair + 1)
                if i % 2 == 0 and not (is_int(g) and g < PBUF):
                    dve.wait_ge(s_quad, (g - PBUF) // 2 + 1 if is_int(g)
                                else quads(sg) + (i - PBUF) // 2 + 1)
                dve.wait_ge(s_wide, g + 1)
                nc.vector.tensor_tensor(prod[:, i % PBUF, :, :], wide[:, i % 2, :, :],
                                        xk[sg.layer][sg.pp][i % 2][:, :].unsqueeze(1)
                                        .to_broadcast([128, 2, BLK]), ALU.mult).then_inc(s_prod, 1)

            def one_step(c, st):
                one, two = st.stage(1), st.stage(2)
                for i in range(UNITS if one else 0):
                    products(one, i)
                for i in range(UNITS if two else 0):
                    if UNITS + i == SPLIT_LOW_SLOT and not st.odd and within(st.b, 0, BT - 2):
                        split_low(st.b + 1)
                    products(two, i)
                if is_int(st.s) and st.s == 0:
                    split_low(1)

            run_steps(dve, one_step)

        @block.tensor
        def _(pe):
            mm = nc.tensor.matmul

            def exchange(e):
                if not (is_int(e) and e == 0):
                    pe.wait_ge(s_taken, e)

            def prep_event(e, n, tp, b):
                exchange(e)
                if n == 0:
                    pe.wait_ge(s_low, b + 1)
                for i in range(4):
                    last = nc.tensor.transpose(
                        exch[:, i * NB:(i + 1) * NB],
                        parts[:, 4 * n + i, :, :, :].rearrange("p a b m -> p (a b m)").bitcast(FP32), ident[:, :])
                last.then_inc(s_ev, 1)

            def square_event(e, t, half, pp, tp):
                exchange(e)
                c = pp * 2 * BLK + half * BLK
                mm(exch[:, :], sums[:, t, :], x0[tp][0:64, c:c + BLK], start=True, stop=True).then_inc(s_ev, 1)

            def l0_tile(e_b, t, pair):
                p = 128 if t < SHIFT_TILES - 1 else M
                pe.wait_ge(s_taken, e_b + 1)
                if t == 0 and not (is_int(pair) and pair == 0):
                    pe.wait_ge(s_x[1], pair)
                for half in range(2):
                    last = mm(acc[0][64 * half:64 * half + 64, :], u[0:p, t, :], sq[t % 2][half][0:p, :],
                              start=t == 0, stop=t == SHIFT_TILES - 1)
                last.then_inc(s_l0, 1)

            def repeat_rows(sg, i):
                j, g = i // 2, sg.base + i
                if not (is_int(g) and g < 2):
                    pe.wait_ge(s_prod, g - 1)
                c = sg.pp * 2 * BLK + (i % 2) * BLK
                for r in range(2):
                    last = mm(wide[:, i % 2, r, :], rows[64 * r:64 * r + 64, j, :],
                              x0[sg.tp][64 * r:64 * r + 64, c:c + BLK], start=True, stop=True)
                last.then_inc(s_wide, 1)

            def contract(sg, j, r):
                tile = 2 * j + r
                if r == 0:
                    pe.wait_ge(s_prod, sg.base + 2 * j + 2)
                if tile == 0 and not (is_int(sg.pair) and sg.pair == 0):
                    pe.wait_ge(s_x[sg.layer + 1], sg.pair)
                for half in range(2):
                    last = mm(acc[sg.layer][64 * half:64 * half + 64, :], wk[sg.layer][:, tile, :],
                              prod[:, (2 * j + half) % PBUF, r, :], start=tile == 0, stop=tile == NT - 1)
                if r == 1:
                    last.then_inc(s_quad, 1)

            def mlp1(e, m, b):
                if m == 0:
                    exchange(e)
                    pe.wait_ge(s_zr, 3 * (b + 1))
                c = slice(m * 128, (m + 1) * 128)
                mm(exch[:, c], wt_a[:, c], zr12[:, :], start=True, stop=False)
                mm(exch[:, c], wt_b[:, c], zr3[:, :], start=False, stop=False)
                last = mm(exch[:, c], wt_c[:, c], dense_t[:, bass.ds(b * NB, NB)], start=False, stop=True)
                if m == H1 // 128 - 1:
                    last.then_inc(s_ev, 1)

            def mlp2(e):
                exchange(e)
                for j in range(H2 // 128):
                    for k in range(H1 // 128):
                        last = mm(exch[:, j * NB:(j + 1) * NB], wt2[:, k, j * 128:(j + 1) * 128], h1[:, k, :],
                                  start=k == 0, stop=k == H1 // 128 - 1)
                last.then_inc(s_ev, 1)

            def mlp3(e):
                exchange(e)
                for k in range(H2 // 128):
                    last = mm(exch[0:1, 0:NB], wt3[:, k:k + 1], h2[:, k, :], start=k == 0, stop=k == H2 // 128 - 1)
                last.then_inc(s_ev, 1)

            pe.wait_ge(s_const, 16 * 4)
            pe.wait_ge(s_ones, 1)
            for b in range(BT):
                last = nc.tensor.transpose(wide[0:ND + 1, b // 8, b // 4 % 2, (b % 4) * NB:(b % 4 + 1) * NB],
                                           dense_in[:, b, :], ident[:, :])
            last.then_inc(s_dtr, 1)
            for n in range(PREP):
                prep_event(n, n, 0, 0)
            pe.wait_ge(s_sel, 2)
            pe.wait_ge(s_u, 2)
            for t in range(SHIFT_TILES):
                for half in range(2):
                    square_event(PREP + 2 * t + half, t, half, 0, 0)
                if t:
                    l0_tile(PREP + 2 * t - 1, t - 1, 0)
            l0_tile(PREP + SQUARES - 1, SHIFT_TILES - 1, 0)
            pe.wait_ge(s_dt, 1)
            for i in range(2):
                repeat_rows(peeled(0).stage(1), i)
            pe.wait_ge(s_w12, 16 * 4)
            pe.wait_ge(s_wtop, 16 * 8)

            def one_step(c, st):
                s, b, e = st.s, st.b, st.event
                before, behind = neighbour(c, st, -1), neighbour(c, st, 1)
                stages = [st.stage(1), st.stage(2)]
                prev = before.stage(2) if before else None
                nxt = behind and (behind.stage(1) or behind.stage(2))
                first_square = None
                for slot in range(2 * UNITS):
                    sg, i = stages[slot // UNITS], slot % UNITS
                    lead = prev if slot < UNITS else stages[0]
                    if sg:
                        follow = (stages[1] if slot < UNITS else None) or nxt
                        if i + 2 < UNITS:
                            repeat_rows(sg, i + 2)
                        elif follow:
                            repeat_rows(follow, i + 2 - UNITS)
                    if st.odd and slot in PREP_SLOT and within(b, 0, BT - 2):
                        prep_event(e, PREP_SLOT[slot], st.tile_parity(2), b + 1)
                        e = e + 1
                    if slot in SQ_SLOT and within(s, 0, PAIRS - 2):
                        if first_square is None:
                            first_square = e
                        square_event(e, *SQ_SLOT[slot], st.pair_parity(1), st.tile_parity(1))
                        e = e + 1
                    if st.odd and within(b, 1, BT):
                        if slot in MLP1_SLOT:
                            mlp1(e, MLP1_SLOT[slot], b - 1)
                            if slot == max(MLP1_SLOT):
                                e = e + 1
                        if slot == MLP2_SLOT:
                            mlp2(e)
                            e = e + 1
                        if slot == MLP3_SLOT:
                            mlp3(e)
                            e = e + 1
                    if slot in L0_SLOT and within(s, 0, PAIRS - 2):
                        t = L0_SLOT[slot]
                        l0_tile(first_square + 2 * t + 1, t, s + 1)
                    if i < 2:
                        if lead:
                            contract(lead, UNITS // 2 - 1, i % 2)
                    elif sg:
                        contract(sg, i // 2 - 1, i % 2)

            run_steps(pe, one_step)
            for r in range(2):
                contract(peeled(LAST).stage(2), UNITS // 2 - 1, r)
            e = peeled(PAIRS - 1).event + MLP
            for m in range(H1 // 128):
                mlp1(e, m, BT - 1)
            mlp2(e + 1)
            mlp3(e + 2)


def kernel(**inputs):
    import numpy as _np
    import concourse.bacc as _bacc
    from concourse import mybir as _mybir
    from concourse.bass_utils import run_bass_kernel_spmd as _run

    nc = _bacc.Bacc("TRN2", target_bir_lowering=False, num_devices=1)
    arrays = {}

    def dram(name, a):
        a = _np.ascontiguousarray(a)
        arrays[f"in_{name}"] = a
        return nc.dram_tensor(f"in_{name}", a.shape, _mybir.dt.from_np(a.dtype), kind="ExternalInput").ap()

    args = {n: dram(n, inputs[n]) for n in inputs}

    p = _np.arange(128)[:, None, None]
    j = _np.arange(NT // 2)[None, :, None]
    q = _np.arange(128)[None, None, :]
    sel_rows = (p % M == 4 * j + 2 * (p // 64) + q // 64).astype(_np.float32)
    p, t = p[:64], _np.arange(SHIFT_TILES)[None, :, None]
    shift = 4 * t + q // M
    sel_sums = ((p % M == q % M) | (p % M == (q % M + shift) % M)).astype(_np.float32)
    out = nc.dram_tensor("out_0", (B, 1), FP32, kind="ExternalOutput").ap()
    tower(nc, args["dense_ctx"], args["ids"], [args[f"tbl_{f}"] for f in range(M)],
          args["W_top1"], args["b_top1"], args["W_top2"], args["b_top2"], args["W_top3"],
          args["L0_rec_W0"], args["L0_rec_W1"], args["L0_rec_W2"],
          dram("sel_rows", sel_rows), dram("sel_sums", sel_sums),
          dram("identity", _np.eye(128, dtype=_np.float32)), out)
    r = _run(nc, [arrays], core_ids=[0])
    return r.results[0]["out_0"]
```

```python
from contextlib import ExitStack

import concourse.bass as bass
import numpy as np
from concourse import mybir

FP32 = mybir.dt.float32
F32R = mybir.dt.float32r
I32 = mybir.dt.int32
U32 = mybir.dt.uint32
ACT = mybir.ActivationFunctionType
ALU = mybir.AluOpType
AX = mybir.AxisListType

B, M, D, K = 2048, 32, 16, 64
NB = 128
BT = B // NB
BLK = 512
PAIRS = B * D // (2 * BLK)
H1, H2 = 512, 256
ND = 16
SHIFT_TILES = 5
NT = M * K // 128
DOUBLE = 6
SINGLE = NT - DOUBLE
BANKS = 4
PRODS = 4
BEHIND, AHEAD = 2, 2
PREP = D * NB // BLK
SQUARES = 2 * SHIFT_TILES
MLP = 3

STEP0, UNROLL, LOOPS = 3, 4, 6
LAST = PAIRS

LEAD = 4
SEQUENCE = {1: list(range(NT)), 2: list(range(DOUBLE, NT)) + list(range(DOUBLE))}
ORDER = ([(1, t) for t in SEQUENCE[1][:LEAD]]
         + [x for a, b in zip(SEQUENCE[2][:NT - LEAD], SEQUENCE[1][LEAD:]) for x in ((2, a), (1, b))]
         + [(2, t) for t in SEQUENCE[2][NT - LEAD:]])
SLOTS = len(ORDER)

PREP_SLOT = {1 + e: e for e in range(PREP)}
SQ_SLOT = {6 + 2 * n: (n // 2, n % 2) for n in range(SQUARES)}
L0_SLOT = {10 + 4 * t: t for t in range(SHIFT_TILES)}
MLP1_SLOT = {0: (0, 1), 1: (2, 3)}
MLP2_SLOT, MLP3_SLOT = 3, 5
X3_SLOT, X1_SLOT, X2_SLOT = 2, 27, 30
DENSE_SLOT = 20
SPLIT_HIGH_SLOT, SPLIT_LOW_SLOT = 22, 25


def is_int(x):
    return isinstance(x, int)


def within(x, low, high):
    return not is_int(x) or low <= x <= high


class Step:

    def __init__(self, c, k):
        self.c, self.k = c, k
        self.s = UNROLL * c + (STEP0 + k)
        self.b = 2 * c + (STEP0 + k) // 2
        self.odd = (STEP0 + k) % 2
        evens = self.b + self.odd
        mlps = max(evens - 2, 0) if is_int(evens) else evens - 2
        self.event = (self.b + 1) * (PREP + SQUARES) + evens * SQUARES + mlps * MLP
        if is_int(self.s) and self.s == LAST:
            self.event -= PREP + SQUARES

    def of_parity(self, d):
        return self.c + ((STEP0 + self.k) // 2 + d) // 2 + 1

    def pair_parity(self, d):
        return (STEP0 + self.k + d) % 2

    def tile_parity(self, d=0):
        return ((STEP0 + self.k + d) // 2) % 2

    def at(self, d):
        if is_int(self.s):
            return peeled(self.s + d) if 0 <= self.s + d <= LAST else None
        return Step(self.c, self.k + d)

    def has(self, layer):
        return within(self.s, 0, PAIRS - 1) if layer == 1 else within(self.s, 1, LAST)

    def unit(self, pos):
        d, pos = pos // SLOTS, pos % SLOTS
        step = self.at(d) if d else self
        return Unit(step, pos) if step and step.has(ORDER[pos][0]) else None


class Unit:

    def __init__(self, step, pos):
        self.step = step
        self.layer, self.tile = ORDER[pos]
        d = 0 if self.layer == 1 else -1
        self.pair, self.pp, self.tp = step.s + d, step.pair_parity(d), step.tile_parity(d)
        self.first = self.tile == SEQUENCE[self.layer][0]
        self.last = self.tile == SEQUENCE[self.layer][-1]
        s = step.s
        before = sum(step.has(layer) for layer, _ in ORDER[:pos])
        self.index = (0 if is_int(s) and s == 0 else 2 * NT * s - NT) + before
        self.buf = before % PRODS
        self.place = self.tile - DOUBLE if self.tile >= DOUBLE else SINGLE + DOUBLE * self.pp + self.tile
        self.rows = NT * self.pair + self.tile


def peeled(s):
    return Step((s - STEP0) // UNROLL, (s - STEP0) % UNROLL)


def run_steps(eng, one_step):
    for s in range(STEP0):
        one_step(None, peeled(s))
    with eng.Fori(0, LOOPS) as c:
        for k in range(UNROLL):
            one_step(c, Step(c, k))
    for s in range(STEP0 + UNROLL * LOOPS, LAST + 1):
        one_step(None, peeled(s))


def tower(nc, dense, ids, tables, w_top1, b_top1, w_top2, b_top2, w_top3, w0, w1, w2,
          sel_rows, sel_sums, identity, out):
    with ExitStack() as ctx:
        def sb(name, shape, dt=FP32):
            return ctx.enter_context(nc.sbuf_tensor(name, shape, dt))

        def pb(name, shape):
            return ctx.enter_context(nc.psum_tensor(name, shape, FP32))

        def sem(name):
            return ctx.enter_context(nc.semaphore(name))

        ident = sb("ident", [128, 128])
        ident_r = sb("ident_r", [128, 128], F32R)
        rows = sb("rows", [128, NT // 2, 128], F32R)
        sums = sb("sums", [64, SHIFT_TILES, 128], F32R)
        u = sb("u", [128, SHIFT_TILES, K])
        wk = {1: sb("w1s", [128, NT, K]), 2: sb("w2s", [128, NT, K])}
        wt_a = sb("wt_a", [128, H1])
        wt_b = sb("wt_b", [128, H1])
        wt_c = sb("wt_c", [ND + 1, H1])
        wt2 = sb("wt2", [128, H1 // 128, H2])
        wt3 = sb("wt3", [128, H2 // 128])
        bt2 = sb("bt2", [128, H2 // 128])
        idx = [sb(f"idx{i}", [128, M], I32) for i in range(2)]
        emb = sb("emb", [128, M, D])
        parts = sb("parts", [128, D, 2, 2, M], F32R)
        x0 = [sb(f"x0_{i}", [128, D * NB], F32R) for i in range(2)]
        sq = [sb(f"sq{i}", [128, 2, BLK]) for i in range(2)]
        xk = {l: [sb(f"x{l}_{i}", [128, 2, BLK]) for i in range(2)] for l in (1, 2)}
        x3 = [sb(f"x3_{i}", [128, BLK]) for i in range(2)]
        prod = sb("prod", [128, PRODS, 2, BLK])
        kept = sb("kept", [128, SINGLE + 2 * DOUBLE, 2, BLK])
        mixed = sb("mixed", [128, B])
        dense_t = mixed[64:64 + ND + 1, :]
        y = mixed[96:97, :]
        dense_now = sb("dense_now", [ND + 1, NB])
        z2 = sb("z2", [128, 2, BLK])
        z = {1: [mixed[0:64, i * BLK:(i + 1) * BLK] for i in range(2)], 2: [z2[:, i, :] for i in range(2)]}
        zh23 = sb("zh23", [128, 2, 2 * NB])
        zh = {1: mixed[0:64, 2 * BLK:2 * BLK + 2 * NB], 2: zh23[:, 0, :], 3: zh23[:, 1, :]}
        zr12, zr3 = sb("zr12", [128, NB]), sb("zr3", [128, NB])
        h1 = sb("h1", [128, H1 // 128, NB])
        h2 = sb("h2", [128, H2 // 128, NB])

        def stage(place, p, shape):
            n = int(np.prod(shape))
            flat = kept[0:p, place:place + 2, :, :].rearrange("p s h n -> p (s h n)")[:, 0:n]
            return flat.rearrange("p (a b) -> p a b", b=shape[1])
        rows_raw = stage(0, 128, (NT // 2, 128))
        sums_raw = stage(1, 64, (SHIFT_TILES, 128))
        w0_mh = stage(2, 128, (SHIFT_TILES, K))
        w0_hm = stage(3, 128, (4, K))
        w0_pair = stage(4, 128, (4, K))
        w0_rows = stage(5, M, (M, K))
        w0_cols = stage(7, M, (M, K))
        dense_in = stage(9, 128, (BT, ND + 1))
        w0_sum = sb("w0_sum", [M, 3, K])

        wide = pb("wide", [128, 2, 2, BLK])
        acc = [pb(f"acc{l}", [128, BLK]) for l in range(3)]
        exch = pb("exch", [128, BLK])

        s_ids = [sem(f"ids_loaded{i}") for i in range(2)]
        s_const = sem("consts_loaded")
        s_w0 = sem("w0_loaded")
        s_w12 = sem("w12_loaded")
        s_wtop = sem("wtop_loaded")
        s_gather = sem("gathered")
        s_go = sem("gather_may_start")
        s_sel = sem("selectors_ready")
        s_ones = sem("ones_ready")
        s_prep = sem("w0_steps")
        s_u = sem("u_ready")
        s_dtr = sem("dense_transposed")
        s_dt = sem("dense_t_ready")
        s_high = sem("high_ready")
        s_low = sem("low_ready")
        s_ev = sem("event_ready")
        s_taken = sem("event_taken")
        s_l0 = sem("l0_tile_done")
        s_wide = sem("wide_ready")
        s_prod = sem("prod_ready")
        s_keep = sem("rows_kept")
        s_unit = sem("unit_done")
        s_x = {1: sem("x1_ready"), 2: sem("x2_ready"), 3: sem("x3_ready")}
        s_zm = {1: sem("z1_second"), 2: sem("z2_second")}
        s_z = {1: sem("z1_summed"), 2: sem("z2_summed"), 3: sem("z3_summed")}
        s_half = sem("z_halved")
        s_zr = sem("z_reduced")
        s_dense = sem("dense_now_ready")
        s_y = sem("y_ready")
        s_out = sem("out_stored")

        def bank(e):
            if not (is_int(e) and e < PREP + SQUARES):
                return exch[:, :]
            n = e % (BANKS + 1)
            return wide[:, n // 2, n % 2, :] if n < BANKS else exch[:, :]

        w0_flat = w0.rearrange("m h k -> (m h) k")

        def w0_pieces():
            for s in range(M // 2 + 1):
                t, p = s // 4, 32 * (s % 4)
                for lo, hi, wrap in ((0, M - s, 0), (M - s, M, M)):
                    if hi == lo:
                        continue
                    first = lo * M + lo + s - wrap
                    n = hi - lo
                    yield (w0_mh[p + lo:p + hi, t, :], w0_flat[first:first + (M + 1) * (n - 1) + 1:M + 1, :])
                    if 0 < s < M // 2:
                        first = (lo + s - wrap) * M + lo
                        yield (w0_hm[p + lo:p + hi, t, :],
                               w0_flat[first:first + (M + 1) * (n - 1) + 1:M + 1, :])
        W0_DMAS = len(list(w0_pieces())) + 2

        block = ctx.enter_context(nc.Block())

        @block.sync
        def _(sp):
            def load_ids(b, par):
                sp.dma_start(idx[par][:, :], ids[bass.ds(b * NB, NB), :]).then_inc(s_ids[par], 16)

            load_ids(0, 0)
            load_ids(1, 1)
            sp.dma_start(dense_in[:, :, 0:ND], dense.rearrange("(t p) f -> p t f", p=NB)).then_inc(s_const, 16)
            sp.dma_start(ident[:, :], identity).then_inc(s_const, 16)
            sp.dma_start(rows_raw[:, :, :], sel_rows).then_inc(s_const, 16)
            sp.dma_start(sums_raw[:, :, :], sel_sums).then_inc(s_const, 16)
            for l, w in ((1, w1), (2, w2)):
                for mi in range(2):
                    sp.dma_start(wk[l][64 * mi:64 * mi + 64, :, :],
                                 w.rearrange("(i two) h k -> two h i k", two=2)[mi]).then_inc(s_w12, 16)
            sp.dma_start(wt_a[:, :], w_top1[0:2 * K, :]).then_inc(s_wtop, 16)
            for h in range(2):
                sp.dma_start(wt_b[64 * h:64 * h + 64, :], w_top1[2 * K:3 * K, :]).then_inc(s_wtop, 16)
            sp.dma_start(wt_c[0:ND, :], w_top1[3 * K:3 * K + ND, :]).then_inc(s_wtop, 16)
            sp.dma_start(wt_c[ND:ND + 1, :], b_top1.rearrange("(a n) -> a n", a=1)).then_inc(s_wtop, 16)
            sp.dma_start(wt2[:, :, :], w_top2.rearrange("(k p) n -> p k n", p=128)).then_inc(s_wtop, 16)
            sp.dma_start(wt3[:, :], w_top3.rearrange("(k p) n -> p (k n)", p=128),
                         allow_slow_non_contiguous=True).then_inc(s_wtop, 16)
            sp.dma_start(bt2[:, :], b_top2.rearrange("(k p) -> p k", p=128),
                         allow_slow_non_contiguous=True).then_inc(s_wtop, 16)

            sp.wait_ge(s_gather, 16 * M)
            load_ids(2, 0)

            def tile_traffic(b, par, load):
                if load:
                    sp.wait_ge(s_gather, 16 * M * (b + 2))
                    load_ids(b + 3, 1 - par)
                sp.wait_ge(s_y, b + 1)
                sp.dma_start(out.rearrange("b one -> one b")[:, bass.ds(b * NB, NB)], y[:, bass.ds(b * NB, NB)])\
                    .then_inc(s_out, 16)

            with sp.Fori(0, BT - 4, 2) as b:
                tile_traffic(b, 0, True)
                tile_traffic(b + 1, 1, True)
            for b in range(BT - 4, BT):
                tile_traffic(b, b % 2, b + 3 < BT)
            sp.wait_ge(s_out, 16 * BT)

        @block.gpsimd
        def _(pool):
            def gather(b, par, nth, lo, hi):
                if lo == 0:
                    pool.wait_ge(s_ids[par], 16 * nth)
                    if not is_int(b) or b > 0:
                        pool.wait_ge(s_low, b)
                        pool.wait_ge(s_high, b)
                pool.sem_inc(s_go, 1)
                for m in range(lo, hi):
                    pool.indirect_dma_start(
                        emb[:, m, :], None, tables[m],
                        bass.IndirectOffsetOnAxis(ap=idx[par][:, m:m + 1].bitcast(U32), axis=0)
                    ).then_inc(s_gather, 16)

            def z_of_layer(l, pair, pp, tp, b):
                p = 64 * l
                a_half, b_half = xk[l][pp][0:p, 0, :], xk[l][pp][0:p, 1, :]
                pool.wait_ge(s_x[l], pair + 1)
                if pp == 0:
                    if not is_int(b) or b >= 2:
                        pool.wait_ge(s_half, 3 * (b - 1))
                    pool.tensor_tensor(z[l][tp], a_half, b_half, ALU.add).then_inc(s_z[l], 1)
                else:
                    pool.wait_ge(s_z[l], pair)
                    pool.tensor_tensor(z[l][tp], z[l][tp], a_half, ALU.add).then_inc(s_zm[l], 1)
                    pool.wait_ge(s_zm[l], b + 1)
                    pool.tensor_tensor(z[l][tp], z[l][tp], b_half, ALU.add).then_inc(s_z[l], 1)

            def z_reduce(b, tp):
                pool.wait_ge(s_x[3], 2 * b + 2)
                pool.tensor_tensor(x3[0][:, :], x3[0][:, :], x3[1][:, :], ALU.add).then_inc(s_z[3], 1)
                pool.wait_ge(s_z[1], 2 * b + 2)
                pool.wait_ge(s_z[2], 2 * b + 2)
                pool.wait_ge(s_z[3], b + 1)
                for l, zl in ((1, z[1][tp]), (2, z[2][tp]), (3, x3[0])):
                    pool.tensor_tensor(zh[l], zl[:, 0:2 * NB], zl[:, 2 * NB:4 * NB], ALU.add).then_inc(s_half, 1)
                pool.wait_ge(s_half, 3 * b + 3)
                pool.tensor_tensor(zr12[:, :], zh[2][:, 0:NB], zh[2][:, NB:2 * NB], ALU.add).then_inc(s_zr, 1)
                pool.tensor_tensor(zr3[:, :], zh[3][:, 0:NB], zh[3][:, NB:2 * NB], ALU.add).then_inc(s_zr, 1)
                pool.wait_ge(s_zr, 3 * b + 2)
                pool.tensor_tensor(zr12[0:64, :], zh[1][:, 0:NB], zh[1][:, NB:2 * NB], ALU.add).then_inc(s_zr, 1)
                pool.wait_ge(s_zr, 3 * b + 3)

            pool.memset(dense_in[:, :, ND:ND + 1], 1.0).then_inc(s_ones, 1)
            gather(0, 0, 1, 0, M)
            gather(1, 1, 1, 0, M // 2)
            z_of_layer(1, 0, 0, 0, 0)

            def one_step(c, st):
                s, b = st.s, st.b
                if st.odd:
                    if within(b, 1, BT):
                        z_reduce(b - 1, st.tile_parity(-2))
                    if within(b, 0, BT - 3):
                        gather(b + 2, st.tile_parity(), st.of_parity(2), 0, M // 2)
                else:
                    if within(b, 0, BT - 2):
                        gather(b + 1, st.tile_parity(2), None, M // 2, M)
                    if within(b, 2, BT):
                        pool.wait_ge(s_y, b - 1)
                if within(s, 0, PAIRS - 2):
                    z_of_layer(1, s + 1, st.pair_parity(1), st.tile_parity(1), b + st.odd)
                if within(s, 0, PAIRS - 1):
                    z_of_layer(2, s, st.pair_parity(0), st.tile_parity(), b)

            run_steps(pool, one_step)
            pool.wait_ge(s_y, BT - 1)
            z_reduce(BT - 1, (BT - 1) % 2)

        @block.scalar
        def _(act):
            for dst, src in w0_pieces():
                act.dma_start(dst, src).then_inc(s_w0, 16)
            act.dma_start(w0_rows[:, :, :], w0).then_inc(s_w0, 16)
            act.dma_start(w0_cols[:, :, :], w0.rearrange("m h k -> h m k")).then_inc(s_w0, 16)

            def split_high(b):
                act.wait_ge(s_gather, 16 * M * (b + 1))
                nc.scalar.copy(parts[:, :, :, 0, :],
                               emb[:, :, :].rearrange("p m d -> p d m").unsqueeze(2)
                               .to_broadcast([128, D, 2, M])).then_inc(s_high, 1)

            def prep_event(e, n, tp):
                act.wait_ge(s_ev, e + 1)
                nc.scalar.copy(x0[tp][:, n * BLK:(n + 1) * BLK], bank(e)).then_inc(s_taken, 1)

            def square_event(e, t, half, pair):
                p = 128 if t < SHIFT_TILES - 1 else 32
                if t >= 2:
                    act.wait_ge(s_l0, SHIFT_TILES * pair + t - 1)
                elif not is_int(pair) or pair > 0:
                    act.wait_ge(s_l0, SHIFT_TILES * pair - t)
                act.wait_ge(s_ev, e + 1)
                nc.scalar.activation(sq[t % 2][0:p, half, :], bank(e)[0:p, :], ACT.Square).then_inc(s_taken, 1)

            def evacuate(layer, st, d):
                nxt, pair, pp = layer + 1, st.s + d, st.pair_parity(d)
                if layer == 0:
                    act.wait_ge(s_l0, SHIFT_TILES * (pair + 1))
                else:
                    last = (st if layer == 1 else st.at(-1)).unit(ORDER.index((layer, SEQUENCE[layer][-1])))
                    act.wait_ge(s_unit, last.index + 1)
                if nxt == 3:
                    if pp == 0 and not (is_int(pair) and pair < 2):
                        act.wait_ge(s_half, 3 * (st.b - 1))
                    nc.scalar.activation(x3[pp][:, :], acc[2][:, :], ACT.Relu).then_inc(s_x[3], 1)
                    return
                if not is_int(pair) or pair >= 2:
                    user = st.at(-1).unit(ORDER.index((nxt, SEQUENCE[nxt][-1])))
                    act.wait_ge(s_prod, user.index + 1)
                    act.wait_ge(s_z[nxt], pair - 1)
                for half in range(2):
                    for copy in range(2):
                        last = nc.scalar.activation(xk[nxt][pp][64 * copy:64 * copy + 64, half, :],
                                                    acc[layer][64 * half:64 * half + 64, :], ACT.Relu)
                last.then_inc(s_x[nxt], 1)

            def keep_rows(q):
                step = q.step if q.tile >= DOUBLE else q.step.at(-1)
                reader = step and step.unit(ORDER.index((2, q.tile)))
                if reader:
                    act.wait_ge(s_prod, reader.index + 1)
                act.wait_ge(s_wide, q.rows + 1)
                nc.scalar.copy(kept[:, q.place, :, :], wide[:, q.tile % 2, :, :]).then_inc(s_keep, 1)

            def pick_dense(b):
                nc.scalar.copy(dense_now[:, :], dense_t[:, bass.ds(b * NB, NB)]).then_inc(s_dense, 1)

            def mlp_event(e, n, b):
                act.wait_ge(s_ev, e + 1)
                if n == 0:
                    nc.scalar.activation(h1[:, :, :], exch[:, :].rearrange("p (m b) -> p m b", b=NB),
                                         ACT.Relu).then_inc(s_taken, 1)
                elif n == 1:
                    for j in range(H2 // 128):
                        last = nc.scalar.activation(h2[:, j, :], exch[:, j * NB:(j + 1) * NB], ACT.Relu,
                                                    bias=bt2[:, j:j + 1])
                    last.then_inc(s_taken, 1)
                else:
                    nc.scalar.copy(y[:, bass.ds(b * NB, NB)], exch[0:1, 0:NB]).then_inc(s_taken, 1)
                    act.wait_ge(s_taken, e + 1)
                    act.sem_inc(s_y, 1)

            split_high(0)
            for n in range(PREP):
                prep_event(n, n, 0)
            for t in range(SHIFT_TILES):
                for half in range(2):
                    square_event(PREP + 2 * t + half, t, half, 0)
            for i in range(AHEAD):
                keep_rows(peeled(0).unit(i))
            evacuate(0, peeled(0), 0)
            act.wait_ge(s_wtop, 16 * 8)

            def one_step(c, st):
                s, b, e = st.s, st.b, st.event
                for slot in range(SLOTS):
                    if st.odd and slot in PREP_SLOT and within(b, 0, BT - 2):
                        prep_event(e, PREP_SLOT[slot], st.tile_parity(2))
                        e = e + 1
                    if slot in SQ_SLOT and within(s, 0, PAIRS - 2):
                        square_event(e, *SQ_SLOT[slot], s + 1)
                        e = e + 1
                    if not st.odd and within(b, 2, BT):
                        n = {max(MLP1_SLOT): 0, MLP2_SLOT: 1, MLP3_SLOT: 2}.get(slot)
                        if n is not None:
                            mlp_event(e, n, b - 2)
                            e = e + 1
                    if slot == DENSE_SLOT and st.odd and within(b, 1, BT):
                        pick_dense(b - 1)
                    if slot == X3_SLOT and within(s, 2, LAST):
                        evacuate(2, st, -2)
                    if slot == X2_SLOT and within(s, 0, PAIRS - 1):
                        evacuate(1, st, 0)
                    if slot == X1_SLOT and within(s, 0, PAIRS - 2):
                        evacuate(0, st, 1)
                    if slot == SPLIT_HIGH_SLOT and not st.odd and within(b, 0, BT - 2):
                        split_high(b + 1)
                    ahead = st.unit(slot + AHEAD)
                    if ahead and ahead.layer == 1:
                        keep_rows(ahead)

            run_steps(act, one_step)
            act.wait_ge(s_unit, 2 * NT * PAIRS)
            nc.scalar.activation(x3[1][:, :], acc[2][:, :], ACT.Relu).then_inc(s_x[3], 1)
            pick_dense(BT - 1)
            e = peeled(LAST).event + MLP
            for n in range(MLP):
                mlp_event(e + n, n, BT - 1)

        @block.vector
        def _(dve):
            dve.wait_ge(s_const, 16 * 4)
            nc.vector.tensor_copy(rows[:, :, :], rows_raw[:, :, :]).then_inc(s_sel, 1)
            nc.vector.tensor_copy(sums[:, :, :], sums_raw[:, :, :]).then_inc(s_sel, 1)
            nc.vector.tensor_copy(ident_r[:, :], ident[:, :]).then_inc(s_sel, 1)
            dve.wait_ge(s_dtr, 1)
            nc.vector.tensor_copy(dense_t, wide[0:ND + 1, :, :, :].rearrange("p a b c -> p (a b c)"))\
                .then_inc(s_dt, 1)
            dve.wait_ge(s_w0, 16 * W0_DMAS)
            nc.vector.tensor_reduce(w0_sum[:, 0, :], w0_rows[:, :, :].rearrange("p h k -> p k h"), AX.X,
                                    ALU.add).then_inc(s_prep, 1)
            nc.vector.tensor_reduce(w0_sum[:, 1, :], w0_cols[:, :, :].rearrange("p h k -> p k h"), AX.X,
                                    ALU.add).then_inc(s_prep, 1)
            dve.wait_ge(s_prep, 2)
            nc.vector.tensor_tensor(w0_sum[:, 2, :], w0_sum[:, 0, :], w0_sum[:, 1, :], ALU.add).then_inc(s_prep, 1)
            dve.wait_ge(s_prep, 3)
            nc.vector.scalar_tensor_tensor(out=w0_hm[0:M, 0, :], in0=w0_mh[0:M, 0, :], scalar=3.0,
                                           in1=w0_sum[:, 2, :], op0=ALU.mult, op1=ALU.subtract).then_inc(s_prep, 1)
            dve.wait_ge(s_prep, 4)
            nc.vector.tensor_tensor(w0_pair[:, :, :], w0_mh[:, 0:4, :], w0_hm[:, :, :], ALU.add).then_inc(s_prep, 1)
            dve.wait_ge(s_prep, 5)
            nc.vector.tensor_scalar(u[:, 0:4, :], w0_pair[:, :, :], 0.5, None, ALU.mult).then_inc(s_u, 1)
            nc.vector.tensor_scalar(u[0:M, 4, :], w0_mh[0:M, 4, :], 0.5, None, ALU.mult).then_inc(s_u, 1)

            def split_low(b):
                dve.wait_ge(s_high, b + 1)
                nc.vector.tensor_tensor(parts[:, :, :, 1, :],
                                        emb[:, :, :].rearrange("p m d -> p d m").unsqueeze(2)
                                        .to_broadcast([128, D, 2, M]),
                                        parts[:, :, :, 0, :].bitcast(FP32), ALU.subtract).then_inc(s_low, 1)

            split_low(0)

            def products(q):
                if q.first:
                    dve.wait_ge(s_x[q.layer], q.pair + 1)
                if q.layer == 1:
                    dve.wait_ge(s_keep, q.rows + 1)
                if not is_int(q.index) or q.index >= PRODS:
                    dve.wait_ge(s_unit, q.index - PRODS + 1)
                nc.vector.tensor_tensor(prod[:, q.buf, :, :], kept[:, q.place, :, :],
                                        xk[q.layer][q.pp][:, :, :], ALU.mult).then_inc(s_prod, 1)

            def one_step(c, st):
                for slot in range(SLOTS):
                    if slot == SPLIT_LOW_SLOT and not st.odd and within(st.b, 0, BT - 2):
                        split_low(st.b + 1)
                    q = st.unit(slot)
                    if q:
                        products(q)

            run_steps(dve, one_step)

        @block.tensor
        def _(pe):
            mm = nc.tensor.matmul

            def exchange(e):
                if not is_int(e) or e >= PREP + SQUARES:
                    pe.wait_ge(s_taken, e)
                elif e > BANKS:
                    pe.wait_ge(s_taken, e - BANKS)

            def prep_event(e, n, tp, b):
                exchange(e)
                if n == 0:
                    pe.wait_ge(s_low, b + 1)
                for i in range(4):
                    last = mm(bank(e)[:, i * NB:(i + 1) * NB],
                              parts[:, 4 * n + i, :, :, :].rearrange("p a b m -> p (a b m)"), ident_r[:, :],
                              start=True, stop=True)
                last.then_inc(s_ev, 1)

            def square_event(e, t, half, pp, tp):
                exchange(e)
                c = pp * 2 * BLK + half * BLK
                mm(bank(e), sums[:, t, :], x0[tp][0:64, c:c + BLK], start=True, stop=True).then_inc(s_ev, 1)

            def l0_tile(e_b, t, pair):
                p = 128 if t < SHIFT_TILES - 1 else M
                pe.wait_ge(s_taken, e_b + 1)
                if t == 0 and not (is_int(pair) and pair == 0):
                    pe.wait_ge(s_x[1], pair)
                for half in range(2):
                    last = mm(acc[0][64 * half:64 * half + 64, :], u[0:p, t, :], sq[t % 2][0:p, half, :],
                              start=t == 0, stop=t == SHIFT_TILES - 1)
                last.then_inc(s_l0, 1)

            def repeat_rows(q):
                if not is_int(q.rows) or q.rows >= 2:
                    pe.wait_ge(s_keep, q.rows - 1)
                r = q.tile % 2
                for half in range(2):
                    c = q.pp * 2 * BLK + half * BLK
                    last = mm(wide[:, r, half, :], rows[64 * r:64 * r + 64, q.tile // 2, :],
                              x0[q.tp][64 * r:64 * r + 64, c:c + BLK], start=True, stop=True)
                last.then_inc(s_wide, 1)

            def contract(q):
                pe.wait_ge(s_prod, q.index + 1)
                if q.first and not (is_int(q.pair) and q.pair == 0):
                    pe.wait_ge(s_x[q.layer + 1], q.pair)
                for half in range(2):
                    last = mm(acc[q.layer][64 * half:64 * half + 64, :], wk[q.layer][:, q.tile, :],
                              prod[:, q.buf, half, :], start=q.first, stop=q.last)
                last.then_inc(s_unit, 1)

            def mlp1(e, chunks, b):
                if 0 in chunks:
                    exchange(e)
                    pe.wait_ge(s_zr, 3 * (b + 1))
                    pe.wait_ge(s_dense, b + 1)
                for m in chunks:
                    c = slice(m * 128, (m + 1) * 128)
                    mm(exch[:, c], wt_a[:, c], zr12[:, :], start=True, stop=False)
                    mm(exch[:, c], wt_b[:, c], zr3[:, :], start=False, stop=False)
                    last = mm(exch[:, c], wt_c[:, c], dense_now[:, :], start=False, stop=True)
                if H1 // 128 - 1 in chunks:
                    last.then_inc(s_ev, 1)

            def mlp2(e):
                exchange(e)
                for j in range(H2 // 128):
                    for k in range(H1 // 128):
                        last = mm(exch[:, j * NB:(j + 1) * NB], wt2[:, k, j * 128:(j + 1) * 128], h1[:, k, :],
                                  start=k == 0, stop=k == H1 // 128 - 1)
                last.then_inc(s_ev, 1)

            def mlp3(e):
                exchange(e)
                for k in range(H2 // 128):
                    last = mm(exch[0:1, 0:NB], wt3[:, k:k + 1], h2[:, k, :], start=k == 0, stop=k == H2 // 128 - 1)
                last.then_inc(s_ev, 1)

            pe.wait_ge(s_const, 16 * 4)
            pe.wait_ge(s_ones, 1)
            for b in range(BT):
                last = nc.tensor.transpose(wide[0:ND + 1, b // 8, b // 4 % 2, (b % 4) * NB:(b % 4 + 1) * NB],
                                           dense_in[:, b, :], ident[:, :])
            last.then_inc(s_dtr, 1)
            pe.wait_ge(s_dt, 1)
            pe.wait_ge(s_sel, 3)
            for n in range(PREP):
                prep_event(n, n, 0, 0)
            pe.wait_ge(s_u, 2)
            pe.wait_ge(s_taken, 2)
            for t in range(SHIFT_TILES):
                for half in range(2):
                    square_event(PREP + 2 * t + half, t, half, 0, 0)
                if t:
                    l0_tile(PREP + 2 * t - 1, t - 1, 0)
            l0_tile(PREP + SQUARES - 1, SHIFT_TILES - 1, 0)
            pe.wait_ge(s_taken, PREP + SQUARES)
            for i in range(AHEAD):
                repeat_rows(peeled(0).unit(i))
            pe.wait_ge(s_w12, 16 * 4)
            pe.wait_ge(s_wtop, 16 * 8)

            def one_step(c, st):
                s, b, e = st.s, st.b, st.event
                first_square = None
                for slot in range(SLOTS):
                    if st.odd and slot in PREP_SLOT and within(b, 0, BT - 2):
                        prep_event(e, PREP_SLOT[slot], st.tile_parity(2), b + 1)
                        e = e + 1
                    if slot in SQ_SLOT and within(s, 0, PAIRS - 2):
                        if first_square is None:
                            first_square = e
                        square_event(e, *SQ_SLOT[slot], st.pair_parity(1), st.tile_parity(1))
                        e = e + 1
                    if not st.odd and within(b, 2, BT):
                        if slot in MLP1_SLOT:
                            mlp1(e, MLP1_SLOT[slot], b - 2)
                            if slot == max(MLP1_SLOT):
                                e = e + 1
                        if slot == MLP2_SLOT:
                            mlp2(e)
                            e = e + 1
                        if slot == MLP3_SLOT:
                            mlp3(e)
                            e = e + 1
                    if slot in L0_SLOT and within(s, 0, PAIRS - 2):
                        t = L0_SLOT[slot]
                        l0_tile(first_square + 2 * t + 1, t, s + 1)
                    behind, ahead = st.unit(slot - BEHIND), st.unit(slot + AHEAD)
                    if behind:
                        contract(behind)
                    if ahead and ahead.layer == 1:
                        repeat_rows(ahead)

            run_steps(pe, one_step)
            for i in range(BEHIND):
                contract(peeled(LAST).unit(SLOTS - BEHIND + i))
            e = peeled(LAST).event + MLP
            for chunks in MLP1_SLOT.values():
                mlp1(e, chunks, BT - 1)
            mlp2(e + 1)
            mlp3(e + 2)


def kernel(**inputs):
    import numpy as _np
    import concourse.bacc as _bacc
    from concourse import mybir as _mybir
    from concourse.bass_utils import run_bass_kernel_spmd as _run

    nc = _bacc.Bacc("TRN2", target_bir_lowering=False, num_devices=1)
    arrays = {}

    def dram(name, a):
        a = _np.ascontiguousarray(a)
        arrays[f"in_{name}"] = a
        return nc.dram_tensor(f"in_{name}", a.shape, _mybir.dt.from_np(a.dtype), kind="ExternalInput").ap()

    args = {n: dram(n, inputs[n]) for n in inputs}

    p = _np.arange(128)[:, None, None]
    j = _np.arange(NT // 2)[None, :, None]
    q = _np.arange(128)[None, None, :]
    sel_rows = (p % M == 4 * j + 2 * (p // 64) + q // 64).astype(_np.float32)
    p, t = p[:64], _np.arange(SHIFT_TILES)[None, :, None]
    shift = 4 * t + q // M
    sel_sums = ((p % M == q % M) | (p % M == (q % M + shift) % M)).astype(_np.float32)
    out = nc.dram_tensor("out_0", (B, 1), FP32, kind="ExternalOutput").ap()
    tower(nc, args["dense_ctx"], args["ids"], [args[f"tbl_{f}"] for f in range(M)],
          args["W_top1"], args["b_top1"], args["W_top2"], args["b_top2"], args["W_top3"],
          args["L0_rec_W0"], args["L0_rec_W1"], args["L0_rec_W2"],
          dram("sel_rows", sel_rows), dram("sel_sums", sel_sums),
          dram("identity", _np.eye(128, dtype=_np.float32)), out)
    r = _run(nc, [arrays], core_ids=[0])
    return r.results[0]["out_0"]
```

```python
from contextlib import ExitStack

import concourse.bass as bass
import numpy as np
from concourse import mybir

FP32 = mybir.dt.float32
F32R = mybir.dt.float32r
I32 = mybir.dt.int32
U32 = mybir.dt.uint32
ACT = mybir.ActivationFunctionType
ALU = mybir.AluOpType

B, M, D, K = 2048, 32, 16, 64
NB = 128
BT = B // NB
BLK = 512
PAIRS = B * D // (2 * BLK)
H1, H2 = 512, 256
ND = 16
SHIFT_TILES = 5
FOLD = 128 * (SHIFT_TILES - 1) + M
NT = M * K // 128
DOUBLE = 8
SINGLE = NT - DOUBLE
PRODS = 4
BEHIND, AHEAD = 3, 4
REPEATED = list(range(6, NT, 3))
COPIED = [t for t in range(NT) if t not in REPEATED]
FIRST_SINGLE = min(t for t in COPIED if t >= DOUBLE)
MLP = 3

STEP0, UNROLL, LOOPS = 3, 4, 6
LAST = PAIRS

LEAD = 4
SEQUENCE = {1: list(range(NT)), 2: list(range(DOUBLE, NT)) + list(range(DOUBLE))}
ORDER = ([(1, t) for t in SEQUENCE[1][:LEAD]]
         + [x for a, b in zip(SEQUENCE[2][:NT - LEAD], SEQUENCE[1][LEAD:]) for x in ((2, a), (1, b))]
         + [(2, t) for t in SEQUENCE[2][NT - LEAD:]])
SLOTS = len(ORDER)

ROWS_SLOT = {p - AHEAD: p for p, (layer, t) in enumerate(ORDER) if layer == 1 and t in REPEATED}
PREP_SLOT = 0
SQ_SLOT = {5: 0, 11: 1, 15: 2, 17: 3, 23: 4}
L0_SLOT = {9: 0, 14: 1, 19: 2, 22: 3, 27: 4}
SPLIT_HIGH_SLOT, SPLIT_LOW_SLOT = 22, 25
DENSE_SLOT = 20
MLP1_SLOT = {28: (0, 1, 2, 3)}
MLP2_SLOT, MLP3_SLOT = 31, 5
X3_SLOT, X1_SLOT, X2_SLOT = 3, 28, 31

USES = len(REPEATED) + SHIFT_TILES + 1
USES_BEFORE = SHIFT_TILES + 1


def is_int(x):
    return isinstance(x, int)


def within(x, low, high):
    return not is_int(x) or low <= x <= high


class Step:

    def __init__(self, c, k):
        self.c, self.k = c, k
        self.s = UNROLL * c + (STEP0 + k)
        self.b = 2 * c + (STEP0 + k) // 2
        self.odd = (STEP0 + k) % 2
        evens = self.b + self.odd
        if is_int(self.s):
            self.event = 1 + 2 * max(self.b - 1, 0) + max(evens - 2, 0)
        else:
            self.event = 1 + 2 * (self.b - 1) + (evens - 2)
        self.use = USES * self.s + USES_BEFORE
        self.use_parity = (USES * (STEP0 + k) + USES_BEFORE) % 2

    def uses(self, slot):
        n = 0
        for t in range(slot + 1):
            found = []
            if t in ROWS_SLOT and self.unit(ROWS_SLOT[t]):
                found.append(("rows", self.unit(ROWS_SLOT[t])))
            if t in SQ_SLOT and within(self.s, 0, PAIRS - 2):
                found.append(("sums", SQ_SLOT[t]))
            if t == PREP_SLOT and within(self.s, 0, PAIRS - 2):
                found.append(("prep", None))
            n += len(found)
        n -= len(found)
        return [(kind, what, self.use + n + i, (self.use_parity + n + i) % 2)
                for i, (kind, what) in enumerate(found)]

    def use_of(self, kind, slot):
        return [index for k, _, index, _ in self.uses(slot) if k == kind][0]

    def of_parity(self, d):
        return self.c + ((STEP0 + self.k) // 2 + d) // 2 + 1

    def pair_parity(self, d):
        return (STEP0 + self.k + d) % 2

    def tile_parity(self, d=0):
        return ((STEP0 + self.k + d) // 2) % 2

    def at(self, d):
        if is_int(self.s):
            return peeled(self.s + d) if 0 <= self.s + d <= LAST else None
        return Step(self.c, self.k + d)

    def has(self, layer):
        return within(self.s, 0, PAIRS - 1) if layer == 1 else within(self.s, 1, LAST)

    def unit(self, pos):
        d, pos = pos // SLOTS, pos % SLOTS
        step = self.at(d) if d else self
        return Unit(step, pos) if step and step.has(ORDER[pos][0]) else None


class Unit:

    def __init__(self, step, pos):
        self.step, self.pos = step, pos
        self.layer, self.tile = ORDER[pos]
        d = 0 if self.layer == 1 else -1
        self.pair, self.pp = step.s + d, step.pair_parity(d)
        self.first = self.tile == SEQUENCE[self.layer][0]
        self.last = self.tile == SEQUENCE[self.layer][-1]
        s = step.s
        before = sum(step.has(layer) for layer, _ in ORDER[:pos])
        self.index = (0 if is_int(s) and s == 0 else 2 * NT * s - NT) + before
        self.buf = before % PRODS
        self.place = self.tile - DOUBLE if self.tile >= DOUBLE else SINGLE + DOUBLE * self.pp + self.tile


def peeled(s):
    return Step((s - STEP0) // UNROLL, (s - STEP0) % UNROLL)


def run_steps(eng, one_step):
    for s in range(STEP0):
        one_step(None, peeled(s))
    with eng.Fori(0, LOOPS) as c:
        for k in range(UNROLL):
            one_step(c, Step(c, k))
    for s in range(STEP0 + UNROLL * LOOPS, LAST + 1):
        one_step(None, peeled(s))


def tower(nc, dense, ids, tables, w_top1, b_top1, w_top2, b_top2, w_top3, w0, w1, w2,
          sel_rows, sel_sums, sel_fold, identity, x0_rows, out):
    with ExitStack() as ctx:
        def sb(name, shape, dt=FP32):
            return ctx.enter_context(nc.sbuf_tensor(name, shape, dt))

        def pb(name, shape):
            return ctx.enter_context(nc.psum_tensor(name, shape, FP32))

        def sem(name):
            return ctx.enter_context(nc.semaphore(name))

        ident = sb("ident", [128, 128])
        ident_r = sb("ident_r", [128, 128], F32R)
        rows = sb("rows", [2 * M, len(REPEATED), 128], F32R)
        sums = sb("sums", [2 * M, SHIFT_TILES, 128], F32R)
        u = sb("u", [128, SHIFT_TILES, K])
        wk = {1: sb("w1s", [128, NT, K]), 2: sb("w2s", [128, NT, K])}
        wt_a = sb("wt_a", [128, H1])
        wt_b = sb("wt_b", [K + ND + 1, H1])
        wt2 = sb("wt2", [128, H1 // 128, H2])
        wt3 = sb("wt3", [128, H2 // 128])
        bt2 = sb("bt2", [128, H2 // 128])
        idx = [sb(f"idx{i}", [128, M], I32) for i in range(2)]
        emb = sb("emb", [128, M, D])
        parts = sb("parts", [128, D, 2, M], F32R)
        x0 = [sb(f"x0_{i}", [2 * M, 2, BLK], F32R) for i in range(2)]
        sq = [sb(f"sq{i}", [128, 2, BLK]) for i in range(2)]
        xk = {l: [sb(f"x{l}_{i}", [128, 2, BLK]) for i in range(2)] for l in (1, 2)}
        x3 = [sb(f"x3_{i}", [128, BLK]) for i in range(2)]
        fields = sb("fields", [M, 2, BLK])
        prod = sb("prod", [128, PRODS, 2, BLK])
        kept = sb("kept", [128, SINGLE + 2 * DOUBLE, 2, BLK])
        mixed = sb("mixed", [128, B])
        dense_t = mixed[64:64 + ND + 1, :]
        y = mixed[96:97, :]
        z2 = sb("z2", [128, 2, BLK])
        z = {1: [mixed[0:64, i * BLK:(i + 1) * BLK] for i in range(2)], 2: [z2[:, i, :] for i in range(2)]}
        zh23 = sb("zh23", [128, 2, 2 * NB])
        zh = {1: mixed[0:64, 2 * BLK:2 * BLK + 2 * NB], 2: zh23[:, 0, :], 3: zh23[:, 1, :]}
        zr12, zr3, z3b = sb("zr12", [128, NB]), sb("zr3", [128, NB]), sb("z3b", [K, NB])
        z3_dense = sb("z3_dense", [K + ND + 1, NB])
        h1 = sb("h1", [128, H1 // 128, NB])
        h2 = sb("h2", [128, H2 // 128, NB])

        def stage(place, p, shape):
            n = int(np.prod(shape))
            flat = kept[0:p, place:place + -(-n // (2 * BLK)), :, :].rearrange("p s h n -> p (s h n)")[:, 0:n]
            return flat.rearrange("p (a b) -> p a b", b=shape[1])
        rows_raw = stage(0, 2 * M, (len(REPEATED), 128))
        sums_raw = stage(1, 2 * M, (SHIFT_TILES, 128))
        w0_in = stage(2, 128, (M * M // 128, K))
        dense_in = stage(3, 128, (BT, ND + 1))
        fold = stage(4, 128, (M * M // 128, FOLD))

        wide = pb("wide", [128, 2, 2, BLK])
        acc = [pb(f"acc{l}", [128, BLK]) for l in range(3)]
        exch = pb("exch", [128, BLK])

        WTOP_DMAS = 6
        s_ids = [sem(f"ids_loaded{i}") for i in range(2)]
        s_const = sem("consts_loaded")
        s_w0 = sem("w0_loaded")
        s_w12 = sem("w12_loaded")
        s_wtop = sem("wtop_loaded")
        s_gather = sem("gathered")
        s_go = sem("gather_may_start")
        s_sel = sem("selectors_ready")
        s_ones = sem("ones_ready")
        s_dtr = sem("dense_transposed")
        s_dt = sem("dense_t_ready")
        s_high = sem("high_ready")
        s_low = sem("low_ready")
        s_ev = sem("event_ready")
        s_taken = sem("event_taken")
        s_l0 = sem("l0_tile_done")
        s_wide = sem("wide_ready")
        s_took = sem("wide_taken")
        s_copied = {t: sem(f"rows_copied{t}") for t in COPIED}
        s_stored = sem("fields_stored")
        s_carry = sem("fields_seen")
        s_prod = sem("prod_ready")
        s_unit = sem("unit_done")
        s_x = {1: sem("x1_ready"), 2: sem("x2_ready"), 3: sem("x3_ready")}
        s_half_a = {1: sem("z1_half_a_added"), 2: sem("z2_half_a_added")}
        s_z = {1: sem("z1_summed"), 2: sem("z2_summed"), 3: sem("z3_summed")}
        s_half = sem("z_halved")
        s_zr = sem("z_reduced")
        s_z3b = sem("z3_moved")
        s_z3 = sem("z3_joined")
        s_dense = sem("dense_picked")
        s_y = sem("y_ready")
        s_out = sem("out_stored")

        block = ctx.enter_context(nc.Block())

        @block.sync
        def _(sp):
            def load_ids(b, par):
                sp.dma_start(idx[par][:, :], ids[bass.ds(b * NB, NB), :]).then_inc(s_ids[par], 16)

            load_ids(0, 0)
            load_ids(1, 1)
            sp.dma_start(dense_in[:, :, 0:ND], dense.rearrange("(t p) f -> p t f", p=NB)).then_inc(s_const, 16)
            sp.dma_start(ident[:, :], identity).then_inc(s_const, 16)
            sp.dma_start(sums_raw[:, :, :], sel_sums).then_inc(s_const, 16)
            sp.dma_start(rows_raw[:, :, :], sel_rows).then_inc(s_const, 16)
            for l, w in ((1, w1), (2, w2)):
                for mi in range(2):
                    sp.dma_start(wk[l][64 * mi:64 * mi + 64, :, :],
                                 w.rearrange("(i two) h k -> two h i k", two=2)[mi]).then_inc(s_w12, 16)
            sp.dma_start(wt_a[:, :], w_top1[0:2 * K, :]).then_inc(s_wtop, 16)
            sp.dma_start(wt_b[0:K + ND, :], w_top1[2 * K:3 * K + ND, :]).then_inc(s_wtop, 16)
            sp.dma_start(wt_b[K + ND:K + ND + 1, :], b_top1.rearrange("(a n) -> a n", a=1)).then_inc(s_wtop, 16)
            sp.dma_start(wt2[:, :, :], w_top2.rearrange("(k p) n -> p k n", p=128)).then_inc(s_wtop, 16)
            sp.dma_start(wt3[:, :], w_top3.rearrange("(k p) n -> p (k n)", p=128),
                         allow_slow_non_contiguous=True).then_inc(s_wtop, 16)
            sp.dma_start(bt2[:, :], b_top2.rearrange("(k p) -> p k", p=128),
                         allow_slow_non_contiguous=True).then_inc(s_wtop, 16)

            def copy_rows(pair, pp, reader, t):
                if reader:
                    sp.wait_ge(s_prod, reader.index + 1)
                place = t - DOUBLE if t >= DOUBLE else SINGLE + DOUBLE * pp + t
                for r in range(2):
                    sp.dma_start(kept[64 * r:64 * r + 64, place, :, :],
                                 x0_rows[pp, 2 * t + r:2 * t + r + 1, :, :].to_broadcast([64, 2, BLK]))\
                        .then_inc(s_copied[t], 16)

            def store_fields(pair, pp, index):
                sp.wait_ge(s_took, index + 1)
                sp.dma_start(x0_rows[pp], fields[:, :, :]).then_inc(s_stored, 16)

            def await_fields(pair):
                sp.wait_ge(s_stored, 16 * (pair + 1))
                sp.sem_inc(s_carry, 1)

            store_fields(0, 0, 1)
            await_fields(0)
            for t in COPIED:
                if t < DOUBLE:
                    copy_rows(0, 0, None, t)

            def one_step(c, st):
                s, b = st.s, st.b
                if not st.odd:
                    if within(b, 2, BT):
                        sp.wait_ge(s_y, b - 1)
                        store(b - 2)
                    if within(b, 0, BT - 3):
                        sp.wait_ge(s_gather, 16 * M * (b + 1))
                        load_ids(b + 2, st.tile_parity())
                for t in COPIED:
                    if t >= DOUBLE and within(s, 0, PAIRS - 1):
                        copy_rows(s, st.pair_parity(0), st.unit(ORDER.index((2, t))), t)
                    if t == FIRST_SINGLE and within(s, 0, PAIRS - 2):
                        store_fields(s + 1, st.pair_parity(1), st.use_of("sums", min(SQ_SLOT)))
                if within(s, 0, PAIRS - 2):
                    await_fields(s + 1)
                    for t in COPIED:
                        if t < DOUBLE:
                            copy_rows(s + 1, st.pair_parity(1), st.unit(ORDER.index((2, t))), t)

            def store(b):
                sp.dma_start(out.rearrange("b one -> one b")[:, bass.ds(b * NB, NB)], y[:, bass.ds(b * NB, NB)])\
                    .then_inc(s_out, 16)

            run_steps(sp, one_step)
            sp.wait_ge(s_y, BT)
            store(BT - 1)
            sp.wait_ge(s_out, 16 * BT)

        @block.gpsimd
        def _(pool):
            def gather(b, par, nth, lo, hi):
                if lo == 0:
                    pool.wait_ge(s_ids[par], 16 * nth)
                    if not is_int(b) or b > 0:
                        pool.wait_ge(s_low, b)
                        pool.wait_ge(s_high, b)
                pool.sem_inc(s_go, 1)
                for m in range(lo, hi):
                    pool.indirect_dma_start(
                        emb[:, m, :], None, tables[m],
                        bass.IndirectOffsetOnAxis(ap=idx[par][:, m:m + 1].bitcast(U32), axis=0)
                    ).then_inc(s_gather, 16)

            def z_of_layer(l, pair, pp, tp, b):
                p = 64 * l
                a_half, b_half = xk[l][pp][0:p, 0, :], xk[l][pp][0:p, 1, :]
                pool.wait_ge(s_x[l], pair + 1)
                if pp == 0:
                    if not is_int(b) or b >= 2:
                        pool.wait_ge(s_half, 3 * (b - 1))
                    pool.tensor_tensor(z[l][tp], a_half, b_half, ALU.add).then_inc(s_z[l], 1)
                else:
                    pool.wait_ge(s_z[l], pair)
                    pool.tensor_tensor(z[l][tp], z[l][tp], a_half, ALU.add).then_inc(s_half_a[l], 1)
                    pool.wait_ge(s_half_a[l], b + 1)
                    pool.tensor_tensor(z[l][tp], z[l][tp], b_half, ALU.add).then_inc(s_z[l], 1)

            def z_reduce(b, tp):
                pool.wait_ge(s_z[1], 2 * b + 2)
                pool.wait_ge(s_z[2], 2 * b + 2)
                for l in (1, 2):
                    pool.tensor_tensor(zh[l], z[l][tp][:, 0:2 * NB], z[l][tp][:, 2 * NB:4 * NB], ALU.add)\
                        .then_inc(s_half, 1)
                pool.wait_ge(s_half, 3 * b + 2)
                pool.tensor_tensor(zr12[:, :], zh[2][:, 0:NB], zh[2][:, NB:2 * NB], ALU.add).then_inc(s_zr, 1)
                pool.wait_ge(s_zr, 3 * b + 1)
                pool.tensor_tensor(zr12[0:64, :], zh[1][:, 0:NB], zh[1][:, NB:2 * NB], ALU.add).then_inc(s_zr, 1)
                pool.wait_ge(s_x[3], 2 * b + 2)
                pool.tensor_tensor(x3[0][:, :], x3[0][:, :], x3[1][:, :], ALU.add).then_inc(s_z[3], 1)
                pool.wait_ge(s_z[3], b + 1)
                pool.tensor_tensor(zh[3], x3[0][:, 0:2 * NB], x3[0][:, 2 * NB:4 * NB], ALU.add).then_inc(s_half, 1)
                pool.wait_ge(s_half, 3 * b + 3)
                pool.tensor_tensor(zr3[:, :], zh[3][:, 0:NB], zh[3][:, NB:2 * NB], ALU.add).then_inc(s_zr, 1)
                pool.wait_ge(s_zr, 3 * b + 3)

            def join_z3(b):
                pool.wait_ge(s_z3b, b + 1)
                pool.tensor_tensor(z3_dense[0:K, :], zr3[0:K, :], z3b[:, :], ALU.add).then_inc(s_z3, 1)

            pool.memset(dense_in[:, :, ND:ND + 1], 1.0).then_inc(s_ones, 1)
            gather(0, 0, 1, 0, M)
            gather(1, 1, 1, 0, M // 2)
            z_of_layer(1, 0, 0, 0, 0)

            def one_step(c, st):
                s, b = st.s, st.b
                if st.odd:
                    if within(b, 1, BT):
                        z_reduce(b - 1, st.tile_parity(-2))
                    if within(b, 0, BT - 3):
                        gather(b + 2, st.tile_parity(), st.of_parity(2), 0, M // 2)
                    if within(b, 1, BT):
                        join_z3(b - 1)
                else:
                    if within(b, 0, BT - 2):
                        gather(b + 1, st.tile_parity(2), None, M // 2, M)
                    if within(b, 2, BT):
                        pool.wait_ge(s_y, b - 1)
                if within(s, 0, PAIRS - 2):
                    z_of_layer(1, s + 1, st.pair_parity(1), st.tile_parity(1), b + st.odd)
                if within(s, 0, PAIRS - 1):
                    z_of_layer(2, s, st.pair_parity(0), st.tile_parity(), b)

            run_steps(pool, one_step)
            pool.wait_ge(s_y, BT - 1)
            z_reduce(BT - 1, (BT - 1) % 2)
            join_z3(BT - 1)

        @block.scalar
        def _(act):
            act.dma_start(w0_in[:, :, :], w0.rearrange("m h k -> (m h) k").rearrange("(a p) k -> p a k", p=128))\
                .then_inc(s_w0, 16)
            act.dma_start(fold[:, :, :], sel_fold).then_inc(s_w0, 16)

            def split_high(b):
                act.wait_ge(s_gather, 16 * M * (b + 1))
                nc.scalar.copy(parts[:, :, 0, :], emb[:, :, :].rearrange("p m d -> p d m")).then_inc(s_high, 1)

            def take_x0(index, buf, pp):
                act.wait_ge(s_wide, index + 1)
                nc.scalar.copy(x0[pp][:, :, :], wide[0:2 * M, buf, :, :]).then_inc(s_took, 1)

            def square(index, buf, t, pair):
                p = 128 if t < SHIFT_TILES - 1 else M
                if t >= 2:
                    act.wait_ge(s_l0, SHIFT_TILES * pair + t - 1)
                elif not is_int(pair) or pair > 0:
                    act.wait_ge(s_l0, SHIFT_TILES * pair - t)
                act.wait_ge(s_wide, index + 1)
                if t == 0:
                    if not is_int(pair) or pair > 0:
                        act.wait_ge(s_stored, 16 * pair)
                    nc.scalar.copy(fields[:, :, :], wide[0:M, buf, :, :])
                nc.scalar.activation(sq[t % 2][0:p, :, :], wide[0:p, buf, :, :], ACT.Square).then_inc(s_took, 1)

            def evacuate(layer, st, d):
                nxt, pair, pp = layer + 1, st.s + d, st.pair_parity(d)
                if layer == 0:
                    act.wait_ge(s_l0, SHIFT_TILES * (pair + 1))
                else:
                    last = (st if layer == 1 else st.at(-1)).unit(ORDER.index((layer, SEQUENCE[layer][-1])))
                    act.wait_ge(s_unit, last.index + 1)
                if nxt == 3:
                    if pp == 0 and not (is_int(pair) and pair < 2):
                        act.wait_ge(s_half, 3 * (st.b - 1))
                    nc.scalar.activation(x3[pp][:, :], acc[2][:, :], ACT.Relu).then_inc(s_x[3], 1)
                    return
                if not is_int(pair) or pair >= 2:
                    user = st.at(-1).unit(ORDER.index((nxt, SEQUENCE[nxt][-1])))
                    act.wait_ge(s_prod, user.index + 1)
                    act.wait_ge(s_z[nxt], pair - 1)
                for half in range(2):
                    for copy in range(2):
                        last = nc.scalar.activation(xk[nxt][pp][64 * copy:64 * copy + 64, half, :],
                                                    acc[layer][64 * half:64 * half + 64, :], ACT.Relu)
                last.then_inc(s_x[nxt], 1)

            def keep_rows(index, buf, q):
                step = q.step if q.tile >= DOUBLE else q.step.at(-1)
                reader = step and step.unit(ORDER.index((2, q.tile)))
                if reader:
                    act.wait_ge(s_prod, reader.index + 1)
                act.wait_ge(s_wide, index + 1)
                nc.scalar.copy(kept[:, q.place, :, :], wide[:, buf, :, :]).then_inc(s_took, 1)

            def mlp_inputs(b):
                nc.scalar.copy(z3_dense[K:K + ND + 1, :], dense_t[:, bass.ds(b * NB, NB)]).then_inc(s_dense, 1)
                act.wait_ge(s_zr, 3 * b + 3)
                nc.scalar.copy(z3b[:, :], zr3[K:2 * K, :]).then_inc(s_z3b, 1)

            def mlp_event(e, n, b):
                act.wait_ge(s_ev, e + 1)
                if n == 0:
                    nc.scalar.activation(h1[:, :, :], exch[:, :].rearrange("p (m b) -> p m b", b=NB),
                                         ACT.Relu).then_inc(s_taken, 1)
                elif n == 1:
                    for j in range(H2 // 128):
                        last = nc.scalar.activation(h2[:, j, :], exch[:, j * NB:(j + 1) * NB], ACT.Relu,
                                                    bias=bt2[:, j:j + 1])
                    last.then_inc(s_taken, 1)
                else:
                    nc.scalar.copy(y[:, bass.ds(b * NB, NB)], exch[0:1, 0:NB]).then_inc(s_taken, 1)
                    act.wait_ge(s_taken, e + 1)
                    act.sem_inc(s_y, 1)

            split_high(0)
            act.wait_ge(s_ev, 1)
            nc.scalar.copy(u[:, 0:SHIFT_TILES - 1, :],
                           exch[:, 0:(SHIFT_TILES - 1) * K].rearrange("p (t k) -> p t k", k=K))
            nc.scalar.copy(u[0:M, SHIFT_TILES - 1, :],
                           exch[0:M, (SHIFT_TILES - 1) * K:SHIFT_TILES * K]).then_inc(s_taken, 1)
            take_x0(0, 0, 0)
            for t in range(SHIFT_TILES):
                square(1 + t, (1 + t) % 2, t, 0)
            evacuate(0, peeled(0), 0)
            act.wait_ge(s_wtop, 16 * WTOP_DMAS)

            def one_step(c, st):
                s, b, e = st.s, st.b, st.event
                for slot in range(SLOTS):
                    for kind, what, index, buf in st.uses(slot):
                        if kind == "rows":
                            keep_rows(index, buf, what)
                        elif kind == "sums":
                            square(index, buf, what, s + 1)
                        else:
                            take_x0(index, buf, st.pair_parity(1))
                    if slot == SPLIT_HIGH_SLOT and not st.odd and within(b, 0, BT - 2):
                        split_high(b + 1)
                    if st.odd and within(b, 1, BT):
                        if slot == DENSE_SLOT:
                            mlp_inputs(b - 1)
                        if slot in (max(MLP1_SLOT), MLP2_SLOT):
                            mlp_event(e, int(slot == MLP2_SLOT), b - 1)
                            e = e + 1
                    if not st.odd and slot == MLP3_SLOT and within(b, 2, BT):
                        mlp_event(e, 2, b - 2)
                        e = e + 1
                    if slot == X3_SLOT and within(s, 2, LAST):
                        evacuate(2, st, -2)
                    if slot == X1_SLOT and within(s, 0, PAIRS - 2):
                        evacuate(0, st, 1)
                    if slot == X2_SLOT and within(s, 0, PAIRS - 1):
                        evacuate(1, st, 0)

            run_steps(act, one_step)
            act.wait_ge(s_unit, 2 * NT * PAIRS)
            nc.scalar.activation(x3[1][:, :], acc[2][:, :], ACT.Relu).then_inc(s_x[3], 1)
            mlp_inputs(BT - 1)
            e = peeled(LAST).event + 1
            for n in range(MLP):
                mlp_event(e + n, n, BT - 1)

        @block.vector
        def _(dve):
            dve.wait_ge(s_const, 16 * 4)
            nc.vector.tensor_copy(sums[:, :, :], sums_raw[:, :, :]).then_inc(s_sel, 1)
            nc.vector.tensor_copy(rows[:, :, :], rows_raw[:, :, :]).then_inc(s_sel, 1)
            nc.vector.tensor_copy(ident_r[:, :], ident[:, :]).then_inc(s_sel, 1)
            dve.wait_ge(s_dtr, 1)
            nc.vector.tensor_copy(dense_t, wide[0:ND + 1, :, :, :].rearrange("p a b c -> p (a b c)"))\
                .then_inc(s_dt, 1)

            def split_low(b):
                dve.wait_ge(s_high, b + 1)
                nc.vector.tensor_tensor(parts[:, :, 1, :], emb[:, :, :].rearrange("p m d -> p d m"),
                                        parts[:, :, 0, :].bitcast(FP32), ALU.subtract).then_inc(s_low, 1)

            split_low(0)

            def products(q):
                if q.first:
                    dve.wait_ge(s_x[q.layer], q.pair + 1)
                if q.layer == 1 and q.tile in COPIED:
                    dve.wait_ge(s_copied[q.tile], 32 * (q.pair + 1))
                elif q.layer == 1:
                    dve.wait_ge(s_took, q.step.use_of("rows", q.pos - AHEAD) + 1)
                if not is_int(q.index) or q.index >= PRODS:
                    dve.wait_ge(s_unit, q.index - PRODS + 1)
                nc.vector.tensor_tensor(prod[:, q.buf, :, :], kept[:, q.place, :, :],
                                        xk[q.layer][q.pp][:, :, :], ALU.mult).then_inc(s_prod, 1)

            def one_step(c, st):
                for slot in range(SLOTS):
                    if slot == SPLIT_LOW_SLOT and not st.odd and within(st.b, 0, BT - 2):
                        split_low(st.b + 1)
                    q = st.unit(slot)
                    if q:
                        products(q)

            run_steps(dve, one_step)

        @block.tensor
        def _(pe):
            mm = nc.tensor.matmul

            def exchange(e):
                pe.wait_ge(s_taken, e)

            def buffer(index):
                if not is_int(index) or index >= 2:
                    pe.wait_ge(s_took, index - 1)

            def transpose(index, buf, pp, b):
                buffer(index)
                if pp == 0:
                    pe.wait_ge(s_low, b + 1)
                for i in range(D // 2):
                    last = mm(wide[0:2 * M, buf, i // 4, i % 4 * NB:(i % 4 + 1) * NB],
                              parts[:, D // 2 * pp + i, :, :].rearrange("p a m -> p (a m)"), ident_r[:, :],
                              start=True, stop=True)
                last.then_inc(s_wide, 1)

            def sum_fields(index, buf, t, pp):
                buffer(index)
                for half in range(2):
                    last = mm(wide[:, buf, half, :], sums[:, t, :], x0[pp][:, half, :],
                              start=True, stop=True)
                last.then_inc(s_wide, 1)

            def l0_tile(index, t, pair):
                p = 128 if t < SHIFT_TILES - 1 else M
                pe.wait_ge(s_took, index + 1)
                if t == 0 and not (is_int(pair) and pair == 0):
                    pe.wait_ge(s_x[1], pair)
                for half in range(2):
                    last = mm(acc[0][64 * half:64 * half + 64, :], u[0:p, t, :], sq[t % 2][0:p, half, :],
                              start=t == 0, stop=t == SHIFT_TILES - 1)
                last.then_inc(s_l0, 1)

            def repeat_rows(index, buf, q):
                buffer(index)
                for half in range(2):
                    last = mm(wide[:, buf, half, :], rows[:, REPEATED.index(q.tile), :],
                              x0[q.pp][:, half, :], start=True, stop=True)
                last.then_inc(s_wide, 1)

            def contract(q):
                pe.wait_ge(s_prod, q.index + 1)
                if q.first and not (is_int(q.pair) and q.pair == 0):
                    pe.wait_ge(s_x[q.layer + 1], q.pair)
                for half in range(2):
                    last = mm(acc[q.layer][64 * half:64 * half + 64, :], wk[q.layer][:, q.tile, :],
                              prod[:, q.buf, half, :], start=q.first, stop=q.last)
                last.then_inc(s_unit, 1)

            def mlp1(e, chunks, b):
                if 0 in chunks:
                    exchange(e)
                    pe.wait_ge(s_zr, 3 * (b + 1))
                    pe.wait_ge(s_z3, b + 1)
                    pe.wait_ge(s_dense, b + 1)
                for m in chunks:
                    c = slice(m * 128, (m + 1) * 128)
                    mm(exch[:, c], wt_a[:, c], zr12[:, :], start=True, stop=False)
                    last = mm(exch[:, c], wt_b[:, c], z3_dense[:, :], start=False, stop=True)
                if H1 // 128 - 1 in chunks:
                    last.then_inc(s_ev, 1)

            def mlp2(e):
                exchange(e)
                for j in range(H2 // 128):
                    for k in range(H1 // 128):
                        last = mm(exch[:, j * NB:(j + 1) * NB], wt2[:, k, j * 128:(j + 1) * 128], h1[:, k, :],
                                  start=k == 0, stop=k == H1 // 128 - 1)
                last.then_inc(s_ev, 1)

            def mlp3(e):
                exchange(e)
                for k in range(H2 // 128):
                    last = mm(exch[0:1, 0:NB], wt3[:, k:k + 1], h2[:, k, :], start=k == 0, stop=k == H2 // 128 - 1)
                last.then_inc(s_ev, 1)

            pe.wait_ge(s_const, 16 * 4)
            pe.wait_ge(s_ones, 1)
            for b in range(BT):
                last = nc.tensor.transpose(wide[0:ND + 1, b // 8, b // 4 % 2, (b % 4) * NB:(b % 4 + 1) * NB],
                                           dense_in[:, b, :], ident[:, :])
            last.then_inc(s_dtr, 1)
            pe.wait_ge(s_w0, 16 * 2)
            for t in range(SHIFT_TILES):
                p = 128 if t < SHIFT_TILES - 1 else M
                for a in range(M * M // 128):
                    last = mm(exch[0:p, t * K:(t + 1) * K], fold[:, a, t * 128:t * 128 + p], w0_in[:, a, :],
                              start=a == 0, stop=a == M * M // 128 - 1)
            last.then_inc(s_ev, 1)
            pe.wait_ge(s_sel, 3)
            pe.wait_ge(s_dt, 1)
            transpose(0, 0, 0, 0)
            pe.wait_ge(s_took, 1)
            pe.wait_ge(s_taken, 1)
            for t in range(SHIFT_TILES):
                sum_fields(1 + t, (1 + t) % 2, t, 0)
                if t:
                    l0_tile(t, t - 1, 0)
            l0_tile(SHIFT_TILES, SHIFT_TILES - 1, 0)
            pe.wait_ge(s_w12, 16 * 4)
            pe.wait_ge(s_wtop, 16 * WTOP_DMAS)

            def one_step(c, st):
                s, b, e = st.s, st.b, st.event
                for slot in range(SLOTS):
                    behind = st.unit(slot - BEHIND)
                    if behind:
                        contract(behind)
                    if slot in L0_SLOT and within(s, 0, PAIRS - 2):
                        t = L0_SLOT[slot]
                        l0_tile(st.use_of("sums", [x for x in SQ_SLOT if SQ_SLOT[x] == t][0]), t, s + 1)
                    if slot == min(SQ_SLOT) and within(s, 0, PAIRS - 2):
                        pe.wait_ge(s_took, st.use_of("prep", PREP_SLOT) + 1)
                    for kind, what, index, buf in st.uses(slot):
                        if kind == "rows":
                            repeat_rows(index, buf, what)
                        elif kind == "prep":
                            transpose(index, buf, st.pair_parity(1), b + st.odd)
                        else:
                            sum_fields(index, buf, what, st.pair_parity(1))
                    if st.odd and within(b, 1, BT):
                        if slot in MLP1_SLOT:
                            mlp1(e, MLP1_SLOT[slot], b - 1)
                            if slot == max(MLP1_SLOT):
                                e = e + 1
                        if slot == MLP2_SLOT:
                            mlp2(e)
                            e = e + 1
                    if not st.odd and slot == MLP3_SLOT and within(b, 2, BT):
                        mlp3(e)
                        e = e + 1

            run_steps(pe, one_step)
            for i in range(BEHIND):
                contract(peeled(LAST).unit(SLOTS - BEHIND + i))
            e = peeled(LAST).event + 1
            for chunks in MLP1_SLOT.values():
                mlp1(e, chunks, BT - 1)
            mlp2(e + 1)
            mlp3(e + 2)


def kernel(**inputs):
    import numpy as _np
    import concourse.bacc as _bacc
    from concourse import mybir as _mybir
    from concourse.bass_utils import run_bass_kernel_spmd as _run

    nc = _bacc.Bacc("TRN2", target_bir_lowering=False, num_devices=1)
    arrays = {}

    def dram(name, a):
        a = _np.ascontiguousarray(a)
        arrays[f"in_{name}"] = a
        return nc.dram_tensor(f"in_{name}", a.shape, _mybir.dt.from_np(a.dtype), kind="ExternalInput").ap()

    args = {n: dram(n, inputs[n]) for n in inputs}

    p = _np.arange(2 * M)[:, None, None]
    tile = _np.array(REPEATED)[None, :, None]
    q = _np.arange(128)[None, None, :]
    sel_rows = (p % M == 2 * tile + q // 64).astype(_np.float32)
    t = _np.arange(SHIFT_TILES)[None, :, None]
    shift = 4 * t + q // M
    sel_sums = ((p % M == q % M) | (p % M == (q % M + shift) % M)).astype(_np.float32)
    m, h = _np.arange(M)[:, None, None], _np.arange(M)[None, :, None]
    col = _np.arange(FOLD)[None, None, :]
    shift, a = col // M, col % M
    z = (a + shift) % M
    pair = ((m == a) & (h == z)) | ((m == z) & (h == a) & (shift < M // 2))
    own = 1.0 * ((m == a) & (h == a)) - 0.5 * ((m == a) ^ (h == a))
    sel_fold = _np.where(shift == 0, own, 0.5 * pair).astype(_np.float32)
    sel_fold = sel_fold.reshape(M * M // 128, 128, FOLD).transpose(1, 0, 2)
    x0_rows = nc.dram_tensor("x0_rows", (2, M, 2, BLK), FP32, kind="Internal").ap()
    out = nc.dram_tensor("out_0", (B, 1), FP32, kind="ExternalOutput").ap()
    tower(nc, args["dense_ctx"], args["ids"], [args[f"tbl_{f}"] for f in range(M)],
          args["W_top1"], args["b_top1"], args["W_top2"], args["b_top2"], args["W_top3"],
          args["L0_rec_W0"], args["L0_rec_W1"], args["L0_rec_W2"],
          dram("sel_rows", sel_rows), dram("sel_sums", sel_sums), dram("sel_fold", sel_fold),
          dram("identity", _np.eye(128, dtype=_np.float32)), x0_rows, out)
    r = _run(nc, [arrays], core_ids=[0])
    return r.results[0]["out_0"]
```
